# Optimizing a Trainium2 kernel written in Bass

```python
import numpy as np
import jax
import jax.numpy as jnp

def _softmax(x, axis=-1):
    return jax.nn.softmax(x, axis=axis)

def _gelu(x):
    return jax.nn.gelu(x, approximate=True)

def _silu(x):
    return jax.nn.silu(x)

def _sigmoid(x):
    return jax.nn.sigmoid(x)

def _layernorm(x, axis=-1, eps=1e-05):
    m = jnp.mean(x, axis=axis, keepdims=True)
    v = jnp.var(x, axis=axis, keepdims=True)
    return (x - m) / jnp.sqrt(v + eps)

def _scatter_add(tgt, idx, src, axis=0):
    return tgt.at[idx].add(src)

def _segment_sum(src, seg, n):
    return jax.ops.segment_sum(src, seg, n)
kernel_name = 'mk_gnn_resnorm_d2_gnn_r32_095706'

def setup_inputs(seed: int=0):
    np.random.seed(seed)
    _w = jnp.asarray

    def _rec_inputs():
        import jax
        import jax.numpy as jnp
        _gk = jax.random.key(seed)
        x = -2.644e-07 + 0.002 * jax.random.normal(jax.random.fold_in(_gk, 1), (15625, 64), jnp.float32)
        src = jax.random.randint(jax.random.fold_in(_gk, 2), (250000,), 0, 15625, jnp.int32)
        dst = jnp.minimum((15625 * jax.random.uniform(jax.random.fold_in(_gk, 3), (250000,)) ** 2.0).astype(jnp.int32), 499999)
        _o = jnp.argsort(dst, stable=True)
        src = src[_o]
        dst = dst[_o]
        edge_weight = jax.random.uniform(jax.random.fold_in(_gk, 13), (250000,), jnp.float32, 0.0, 0.999999)
        return (x, src, dst, edge_weight)
    x, src, dst, edge_weight = _rec_inputs()

    def _L0_gnn_setup():
        import jax, jax.numpy as jnp
        import numpy as np
        N_USERS = 9375
        N_ITEMS = 6250
        N = N_USERS + N_ITEMS
        E = 1250000
        DIM = 64
        N_LAYERS = 3
        key = jax.random.key(seed)
        k1, k2, k3 = jax.random.split(key, 3)
        bound = float(np.sqrt(6.0 / (N + DIM)))
        embedding = jax.random.uniform(k1, (N, DIM), dtype=jnp.float32, minval=-bound, maxval=bound)
        edge_index = jax.random.randint(k2, (2, E), 0, N, dtype=jnp.int64)
        edge_weight = jax.random.uniform(k3, (E,), dtype=jnp.float32)
        return {'embedding': embedding, 'edge_index': edge_index, 'edge_weight': edge_weight}
    _L0_gnn_all = _L0_gnn_setup()
    _L0_gnn_in = {k: v for k, v in _L0_gnn_all.items() if k in ()}
    del _L0_gnn_all

    def _L1_gnn_setup():
        import jax, jax.numpy as jnp
        import numpy as np
        N_NODES = 50000
        N_EDGES = 25000
        IN_FEATS = 64
        H_FEATS = 64

        def _sage_conv(h, src, dst, W_self, W_neigh, b, n_nodes):
            agg = jax.ops.segment_sum(h[src], dst, num_segments=n_nodes)
            deg = jax.ops.segment_sum(jnp.ones_like(dst, dtype=h.dtype), dst, num_segments=n_nodes)
            agg = agg / jnp.maximum(deg, 1.0)[:, None]
            return h @ W_self + agg @ W_neigh + b
        key = jax.random.key(seed)
        ks = jax.random.split(key, 8)
        x = jax.random.normal(ks[0], (N_NODES, IN_FEATS), dtype=jnp.float32)
        src = jax.random.randint(ks[1], (N_EDGES,), 0, N_NODES, dtype=jnp.int64)
        dst = jax.random.randint(ks[2], (N_EDGES,), 0, N_NODES, dtype=jnp.int64)
        s1 = 1.0 / np.sqrt(IN_FEATS)
        s2 = 1.0 / np.sqrt(H_FEATS)
        W_self1 = jax.random.normal(ks[3], (IN_FEATS, H_FEATS), dtype=jnp.float32) * s1
        W_neigh1 = jax.random.normal(ks[4], (IN_FEATS, H_FEATS), dtype=jnp.float32) * s1
        b1 = jnp.zeros((H_FEATS,), dtype=jnp.float32)
        W_self2 = jax.random.normal(ks[5], (H_FEATS, H_FEATS), dtype=jnp.float32) * s2
        W_neigh2 = jax.random.normal(ks[6], (H_FEATS, H_FEATS), dtype=jnp.float32) * s2
        b2 = jnp.zeros((H_FEATS,), dtype=jnp.float32)
        return {'x': x, 'src': src, 'dst': dst, 'W_self1': W_self1, 'W_neigh1': W_neigh1, 'b1': b1, 'W_self2': W_self2, 'W_neigh2': W_neigh2, 'b2': b2}
    _L1_gnn_all = _L1_gnn_setup()
    _L1_gnn_in = {k: v for k, v in _L1_gnn_all.items() if k in ('W_self1', 'W_neigh1', 'b1', 'W_self2', 'W_neigh2', 'b2')}
    del _L1_gnn_all
    return {'x': x, 'src': src, 'dst': dst, 'edge_weight': edge_weight, 'L1_gnn_W_self1': _L1_gnn_in['W_self1'], 'L1_gnn_W_neigh1': _L1_gnn_in['W_neigh1'], 'L1_gnn_b1': _L1_gnn_in['b1'], 'L1_gnn_W_self2': _L1_gnn_in['W_self2'], 'L1_gnn_W_neigh2': _L1_gnn_in['W_neigh2'], 'L1_gnn_b2': _L1_gnn_in['b2']}

def reference(x, src, dst, edge_weight, L1_gnn_W_self1, L1_gnn_W_neigh1, L1_gnn_b1, L1_gnn_W_self2, L1_gnn_W_neigh2, L1_gnn_b2):
    import jax
    import jax.numpy as jnp

    def _L0_gnn_ref(embedding, edge_index, edge_weight):
        import jax, jax.numpy as jnp
        import numpy as np
        N_USERS = 9375
        N_ITEMS = 6250
        N = N_USERS + N_ITEMS
        E = 1250000
        DIM = 64
        N_LAYERS = 3
        row, col = (edge_index[0], edge_index[1])
        x = embedding
        acc = embedding
        for _ in range(N_LAYERS):
            msgs = edge_weight[:, None] * x[row]
            x = jax.ops.segment_sum(msgs, col, num_segments=N)
            acc = acc + x
        return acc / jnp.float32(N_LAYERS + 1)

    def _L1_gnn_ref(x, src, dst, W_self1, W_neigh1, b1, W_self2, W_neigh2, b2):
        import jax, jax.numpy as jnp
        import numpy as np
        N_NODES = 50000
        N_EDGES = 25000
        IN_FEATS = 64
        H_FEATS = 64

        def _sage_conv(h, src, dst, W_self, W_neigh, b, n_nodes):
            agg = jax.ops.segment_sum(h[src], dst, num_segments=n_nodes)
            deg = jax.ops.segment_sum(jnp.ones_like(dst, dtype=h.dtype), dst, num_segments=n_nodes)
            agg = agg / jnp.maximum(deg, 1.0)[:, None]
            return h @ W_self + agg @ W_neigh + b
        n = x.shape[0]
        h = _sage_conv(x, src, dst, W_self1, W_neigh1, b1, n)
        h = jax.nn.relu(h)
        h = _sage_conv(h, src, dst, W_self2, W_neigh2, b2, n)
        return h
    edge_index = jnp.stack([src, dst])
    x = _layernorm(x + _L0_gnn_ref(x, edge_index, edge_weight), axis=-1)
    x = _layernorm(x + _L1_gnn_ref(x, src, dst, L1_gnn_W_self1, L1_gnn_W_neigh1, L1_gnn_b1, L1_gnn_W_self2, L1_gnn_W_neigh2, L1_gnn_b2), axis=-1)
    return x

_drawn_inputs = setup_inputs


def setup_inputs(seed=0):
    import zlib

    import numpy as np

    out = dict(_drawn_inputs(seed))
    spreads = {'L1_gnn_b1': (0.0, 0.1), 'L1_gnn_b2': (0.0, 0.1)}
    factors = {}
    for name, (base, spread) in spreads.items():
        noise = np.random.default_rng([zlib.crc32(name.encode()), seed]).standard_normal(out[name].shape)
        drawn = base * np.exp(spread * noise) if base else spread * noise
        out[name] = jnp.asarray(drawn.astype(out[name].dtype))
    for name, factor in factors.items():
        out[name] = (out[name] * factor).astype(out[name].dtype)
    return out
```

```python
from contextlib import ExitStack

import numpy as np

import concourse.bass as bass
from concourse import mybir

F32 = mybir.dt.float32
I32 = mybir.dt.int32
ALU = mybir.AluOpType
ACT = mybir.ActivationFunctionType
AX = mybir.AxisListType

P = 128
N, D, E = 15625, 64, 250000
LIGHT, SAGE = 3, 2
LAYERS = LIGHT + SAGE
EPS = 1e-5

SB = 2
BN = SB * P
NB = -(-N // BN)
DB = 4
G = NB * SB
STEPS = G // DB
NPAD = G * P
ROWS = -(-E // P)
FULL = E // P
LAST = E - FULL * P
ITEMS = -(-(ROWS + NB - 1) // 32) * 32
CHUNKS = -(-ITEMS // P)
SLOTS = CHUNKS * P
RING = 16
BODY = 2 * RING
PACE = 4
LOOKAHEAD = 2
HOTS = 4
BANKS = 4
COUNT_P, COUNT_F = 125, E // 125
NOWHERE = 1 << 20
Q = 4
GQ = G // Q


def build_program(nc, x, src, dst, edge_weight, w_self1, w_neigh1, b1, w_self2, w_neigh2, b2, out):
    table = [nc.dram_tensor(f"table{l}", (NPAD, D), F32, kind="Internal").ap() for l in range(LAYERS)]
    edges = nc.dram_tensor("edges", (SLOTS, 3 * P), I32, kind="Internal").ap()
    edges3 = edges.rearrange("r (a e) -> r a e", a=3)
    layer_rows = [t.rearrange("(p g) d -> p (g d)", p=P) for t in table]

    ctx = ExitStack()
    with ctx:
        def sb(name, shape, dt=F32):
            return ctx.enter_context(nc.sbuf_tensor(name, shape, dt))

        def ps(name, shape, dt=F32):
            return ctx.enter_context(nc.psum_tensor(name, shape, dt))

        def sem(name):
            return ctx.enter_context(nc.semaphore(name))

        base = sb("base", [P, G, D])
        total = sb("total", [P, G, D])
        agg = sb("agg", [P, 2, G, D])
        degree = sb("degree", [P, G])
        src_t = sb("src_t", [P, SLOTS], I32)
        dst_t = sb("dst_t", [P, SLOTS])
        wgt_t = sb("wgt_t", [P, SLOTS])
        group_of = sb("group_of", [1, SLOTS], I32)
        index = sb("index", [P, 2, RING], I32)
        dst_c = sb("dst_c", [P, 2, RING])
        wgt_c = sb("wgt_c", [P, 2, RING])
        msg = sb("msg", [P, RING, D + 1])
        hot = sb("hot", [P, HOTS, BN])
        ident = sb("ident", [P, P])
        ones = sb("ones", [P, P])
        zero = sb("zero", [P, 1])
        iota_i = sb("iota_i", [P, BN], I32)
        weights = sb("weights", [P, 2, D])
        bias = sb("bias", [1, 2, D])
        count = sb("count", [P, NB + 1])
        edge_at = sb("edge_at", [P, NB + 1])
        edge_i = sb("edge_i", [P, NB + 1], I32)
        row_i = sb("row_i", [P, NB + 1], I32)
        row_at = sb("row_at", [P, NB + 1])
        last_f = sb("last_f", [P, NB])
        last_i = sb("last_i", [P, NB], I32)
        some = sb("some", [P, NB])
        rows_of = sb("rows_of", [P, NB])
        item_at = sb("item_at", [P, NB + 1])
        lag = sb("lag", [P, NB])
        slip = sb("slip", [P, NB - 1])
        zeros_b = sb("zeros_b", [P, NB])
        item_i = sb("item_i", [P, CHUNKS], I32)
        item_f = sb("item_f", [P, CHUNKS])
        begun = sb("begun", [P, CHUNKS, NB - 1])
        slips = sb("slips", [P, CHUNKS, NB - 1])
        block_f = sb("block_f", [P, CHUNKS])
        first_dst = sb("first_dst", [P, CHUNKS])
        first_grp = sb("first_grp", [P, CHUNKS])
        shift = sb("shift", [P, CHUNKS])
        row_of = sb("row_of", [P, CHUNKS], I32)
        grp_i = sb("grp_i", [CHUNKS, P], I32)
        pick = sb("pick", [P, 2], I32)
        tail = sb("tail", [SLOTS - FULL, 3, P], I32)
        rows = sb("rows", [P, 2, 3, P], I32)
        low = sb("low", [P, 2, P], I32)
        high = sb("high", [P, 2, P], I32)
        rowf = sb("rowf", [P, 2, 2, P])
        rstd = sb("rstd", [P, G])
        sum_f = sb("sum_f", [P, G])
        rdeg = sb("rdeg", [P, G])
        both = sb("both", [P, 2, DB, 2 * D])
        bothT = sb("bothT", [P, 2, DB * P])
        room = agg[:, 1, :, :].rearrange("p g d -> p (g d)")
        dst_i = room[0:COUNT_P, 0:COUNT_F].bitcast(I32)
        dst_f = room[0:COUNT_P, COUNT_F:2 * COUNT_F]
        below = room[0:COUNT_P, 2 * COUNT_F:3 * COUNT_F]

        iota_p = ps("iota_p", [P, BN])
        sums = [ps(f"sums{i}", [P, SB, D + 1]) for i in range(BANKS)]
        stage = [ps(f"stage{i}", [P, 512]) for i in range(3)]

        s_x, s_dst, s_par, s_tail, s_edges, s_total = (sem(n) for n in ("x_in", "dst_in", "params_in", "tail_in", "edges_out", "total_in"))
        tail_set, iota_set, item_set = sem("tail_set"), sem("iota_set"), sem("item_set")
        dve_chain, ident_set = sem("dve_chain"), sem("ident_set")
        counted, edge_sum, rows_set, grp_ready, grp_T, grp_copied, grp_flat = (
            sem(n) for n in ("counted", "edge_sum", "rows_set", "grp_ready", "grp_T", "grp_copied", "grp_flat"))
        picked, rows_in, row_done, row_T, tab_done = sem("picked"), [sem("rows_in0"), sem("rows_in1")], sem("row_done"), sem("row_T"), sem("tab_done")
        agg_zero = sem("agg_zero")
        layer_in = sem("layer_in")
        idx_ready = sem("idx_ready")
        landed = [sem(f"landed{j}") for j in range(RING)]
        paced = sem("paced")
        slot_free = sem("slot_free")
        cols_ready = sem("cols_ready")
        unweighted = sem("unweighted")
        hot_ready = sem("hot_ready")
        bank_free = sem("bank_free")
        layer_done = sem("layer_done")
        cat_ready, cat_T, catT_ready, dense_done, dense_out = (
            sem(n) for n in ("cat_ready", "cat_T", "catT_ready", "dense_done", "dense_out"))
        catx_ready = sem("catx_ready")
        centred, squared, var_set, std_set, normed = (sem(n) for n in ("centred", "squared", "var_set", "std_set", "normed"))
        s_out, s_low, deg_added, summed = sem("s_out"), sem("row_split"), sem("deg_added"), sem("summed")
        block = ctx.enter_context(nc.Block())

        @block.sync
        def _(sp):
            sp.dma_start(dst_i, dst.rearrange("(p f) -> p f", p=COUNT_P)).then_inc(s_dst, 16)
            whole = N // P
            sp.dma_start(base[:, 0:whole, :], x[0:whole * P, :].rearrange("(g p) d -> p g d", p=P)).then_inc(s_x, 16)
            sp.wait_ge(agg_zero, 1)
            sp.dma_start(base[0:N - whole * P, whole, :], x[whole * P:N, :]).then_inc(s_x, 16)
            for a, arr in enumerate((src, dst, edge_weight.bitcast(I32))):
                sp.dma_start(edges3[0:FULL, a, :], arr[0:FULL * P].rearrange("(r e) -> r e", e=P)).then_inc(s_edges, 16)
            sp.wait_ge(tail_set, 3)
            for a, arr in enumerate((src, dst, edge_weight.bitcast(I32))):
                sp.dma_start(tail[0:1, a, 0:LAST], arr[FULL * P:E].rearrange("(r e) -> r e", r=1)).then_inc(s_tail, 16)
            sp.wait_ge(s_tail, 48)
            sp.dma_start(edges3[FULL:SLOTS, :, :], tail[:, :, :]).then_inc(s_edges, 16)
            for l, (ws, wn, b) in enumerate(((w_self1, w_neigh1, b1), (w_self2, w_neigh2, b2))):
                sp.dma_start(weights[0:D, l, :], ws).then_inc(s_par, 16)
                sp.dma_start(weights[D:2 * D, l, :], wn).then_inc(s_par, 16)
                sp.dma_start(bias[:, l, :], b.rearrange("(r d) -> r d", r=1)).then_inc(s_par, 16)
            sp.wait_ge(s_x, 32)
            sp.dma_start(layer_rows[0], base[:, :, :].rearrange("p g d -> p (g d)")).then_inc(layer_in, 16)
            sp.wait_ge(grp_copied, 1)
            sp.dma_start(group_of[0:1, :].rearrange("r (k p) -> r k p", k=CHUNKS), grp_i[:, :]).then_inc(grp_flat, 16)
            for l in range(LIGHT - 1):
                sp.wait_ge(layer_done, l + 1)
                sp.dma_start(layer_rows[l + 1], agg[:, l, :, :].rearrange("p g d -> p (g d)")).then_inc(layer_in, 16)
            sp.wait_ge(normed, Q)
            sp.dma_start(layer_rows[LIGHT], base[:, :, :].rearrange("p g d -> p (g d)")).then_inc(layer_in, 16)
            sp.wait_ge(dense_out, STEPS + 1)
            sp.dma_start(layer_rows[LIGHT + 1], total[:, :, :].rearrange("p g d -> p (g d)")).then_inc(layer_in, 16)
            for q in range(Q):
                sp.wait_ge(normed, Q + q + 1)
                g0, g1 = q * GQ, min((q + 1) * GQ, whole)
                sp.dma_start(out[g0 * P:g1 * P, :].rearrange("(g p) d -> p g d", p=P), base[:, g0:g1, :]).then_inc(s_out, 16)
            sp.dma_start(out[whole * P:N, :], base[0:N - whole * P, whole, :]).then_inc(s_out, 16)
            sp.wait_ge(layer_in, 16 * LAYERS)
            sp.wait_ge(s_edges, 64)
            sp.wait_ge(s_out, 16 * (Q + 1))

        @block.gpsimd
        def _(pool):
            pool.memset(base[:, N // P:G, :], 0.0).then_inc(agg_zero, 1)
            pool.memset(tail[:, 0, :], 0).then_inc(tail_set, 1)
            pool.memset(tail[:, 1, :], NOWHERE).then_inc(tail_set, 1)
            pool.memset(tail[:, 2, :], 0).then_inc(tail_set, 1)
            pool.iota(iota_i[:, :], [[1, BN]], base=0, channel_multiplier=0).then_inc(iota_set, 1)
            pool.iota(item_i[:, :], [[P, CHUNKS]], base=0, channel_multiplier=1).then_inc(item_set, 1)
            pool.memset(ident[:, :], 0.0).then_inc(ident_set, 1)
            pool.wait_ge(ident_set, 1)
            pool.affine_select(out=ident[:, :], in_=ident[:, :], compare_op=ALU.not_equal, fill=1.0, base=0,
                               pattern=[[-1, P]], channel_multiplier=1).then_inc(ident_set, 1)
            pool.memset(agg[:, 0, :, :], 0.0).then_inc(agg_zero, 1)
            pool.wait_ge(s_edges, 64)
            pool.wait_ge(rows_set, 1)
            with pool.Fori(0, CHUNKS // 2) as pair:
                for h in range(2):
                    k = pair * 2
                    pool.wait_ge(tab_done, k + h + 1)
                    pool.tensor_copy(pick[:, h:h + 1], row_of[:, bass.ds(k + h, 1)]).then_inc(picked, 1)
                    pool.wait_ge(picked, k + h + 1)
                    pool.sem_inc(paced, 1)
                    pool.indirect_dma_start(rows[:, h, :, :].rearrange("p a e -> p (a e)"), None, edges,
                                            bass.IndirectOffsetOnAxis(pick[:, h:h + 1], axis=0)).then_inc(rows_in[h], 16)

            def gather_layer(layer):
                with pool.Fori(0, ITEMS // BODY) as turn:
                    i0 = turn * BODY
                    i = layer * ITEMS + i0
                    pool.wait_ge(layer_in, (layer + 1) * 16)
                    for h in range(2):
                        pool.wait_ge(idx_ready, layer * (ITEMS // RING) + turn * 2 + h + 1)
                        for j in range(RING):
                            if j % PACE == 0:
                                pool.wait_ge(slot_free, i + (h * RING + j + PACE))
                                pool.sem_inc(paced, 1)
                            pool.indirect_dma_start(msg[:, j, 0:D], None, table[layer],
                                                    bass.IndirectOffsetOnAxis(index[:, h, j:j + 1], axis=0)).then_inc(landed[j], 16)

            for l in range(LAYERS):
                gather_layer(l)

        @block.tensor
        def _(pe):
            pe.wait_ge(counted, 1)
            nc.tensor.matmul(stage[0][:, 0:NB + 1], ones[:, :], count[:, :], start=True, stop=True).then_inc(edge_sum, 1)
            pe.wait_ge(grp_ready, 1)
            pe.wait_ge(ident_set, 2)
            nc.tensor.transpose(stage[1][0:CHUNKS, 0:P], first_grp[:, :], ident[:, :]).then_inc(grp_T, 1)
            pe.wait_ge(grp_copied, 1)
            with pe.Fori(0, CHUNKS // 2) as pair:
                for h in range(2):
                    k = pair * 2
                    pe.wait_ge(row_done, k + h + 1)
                    pe.wait_ge(tab_done, k + h + 1)
                    nc.tensor.transpose(stage[h][:, 0:P], rowf[:, h, 0, :], ident[:, :])
                    nc.tensor.transpose(stage[h][:, P:2 * P], rowf[:, h, 1, :], ident[:, :])
                    nc.tensor.transpose(stage[h][:, 2 * P:3 * P], rows[:, h, 2, :].bitcast(F32), ident[:, :]).then_inc(row_T, 1)

            def sum_layer(layer, width):
                with pe.Fori(0, ITEMS // BODY) as turn:
                    i0 = turn * BODY
                    i = layer * ITEMS + i0
                    use = layer * (ITEMS // RING) + turn * 2
                    for j in range(BODY):
                        pe.wait_ge(landed[j % RING], use * 16 + (j // RING + 1) * 16)
                        pe.wait_ge(bank_free, i + (j + 1))
                        pe.wait_ge(hot_ready, i + (j + 1))
                        for g in range(SB):
                            mm = nc.tensor.matmul(sums[j % BANKS][:, g, 0:width], hot[:, j % HOTS, g * P:(g + 1) * P],
                                                  msg[:, j % RING, 0:width], start=True, stop=True)
                        mm.then_inc(slot_free, 1)

            def dense(l):
                with pe.Fori(0, STEPS) as n:
                    t = n + l * STEPS
                    pe.wait_ge(cat_ready, t + 1)
                    pe.wait_ge(catx_ready, t + 1)
                    for g in range(DB):
                        tr = nc.tensor.transpose(stage[0][:, g * P:(g + 1) * P], both[:, 0, g, :], ident[:, :])
                    tr.then_inc(cat_T, 1)
                    pe.wait_ge(catT_ready, t + 1)
                    for g in range(DB):
                        nc.tensor.matmul(stage[1][:, g * D:(g + 1) * D], bothT[:, 0, g * P:(g + 1) * P], weights[:, l, :],
                                         start=True, stop=False)
                        mm = nc.tensor.matmul(stage[1][:, g * D:(g + 1) * D], ones[0:1, :], bias[:, l, :],
                                              start=False, stop=True)
                    mm.then_inc(dense_done, 1)

            with pe.Fori(0, LIGHT) as l:
                sum_layer(l, D)
            sum_layer(LIGHT, D + 1)
            pe.wait_ge(s_par, 96)
            dense(0)
            sum_layer(LIGHT + 1, D)
            dense(1)

        @block.scalar
        def _(act):
            act.wait_ge(s_x, 32)
            nc.scalar.activation(total[:, :, :], base[:, :, :], ACT.Copy).then_inc(s_total, 1)
            act.wait_ge(grp_T, 1)
            nc.scalar.activation(grp_i[:, :], stage[1][0:CHUNKS, 0:P], ACT.Copy).then_inc(grp_copied, 1)
            with act.Fori(0, CHUNKS // 2) as pair:
                for h in range(2):
                    k = pair * 2
                    act.wait_ge(row_T, k + h + 1)
                    cols = bass.ds((k + h) * P, P)
                    nc.scalar.activation(src_t[:, cols], stage[h][:, 0:P], ACT.Copy)
                    nc.scalar.activation(dst_t[:, cols], stage[h][:, P:2 * P], ACT.Copy)
                    nc.scalar.activation(wgt_t[:, cols], stage[h][:, 2 * P:3 * P], ACT.Copy).then_inc(tab_done, 1)
            act.wait_ge(tab_done, 2 + CHUNKS)

            def index_layer(layer):
                with act.Fori(0, ITEMS // BODY) as turn:
                    i0 = turn * BODY
                    i = layer * ITEMS + i0
                    for h in range(2):
                        act.wait_ge(slot_free, i + (h * RING + 1))
                        cols = bass.ds(i0 + h * RING, RING)
                        nc.scalar.activation(index[:, h, :], src_t[:, cols], ACT.Copy).then_inc(idx_ready, 1)
                        nc.scalar.activation(dst_c[:, h, :], dst_t[:, cols], ACT.Copy)
                        nc.scalar.activation(wgt_c[:, h, :], wgt_t[:, cols], ACT.Copy).then_inc(cols_ready, 1)

            def clear(l, parity):
                act.wait_ge(layer_done, l + 1)
                nc.scalar.activation(agg[:, parity, :, :].rearrange("p g d -> p (g d)") if isinstance(parity, int) else
                                     agg[:, bass.ds(parity, 1), :, :].rearrange("p l g d -> p (l g d)"),
                                     zero[:, 0:1].to_broadcast([P, G * D]), ACT.Copy).then_inc(agg_zero, 1)

            def norm():
                for q in range(Q):
                    gs = slice(q * GQ, (q + 1) * GQ)
                    rnd = norms[0] * Q
                    act.wait_ge(centred, rnd + q + 1)
                    nc.scalar.activation(total[:, gs, :], base[:, gs, :], ACT.Square).then_inc(squared, 1)
                for q in range(Q):
                    gs = slice(q * GQ, (q + 1) * GQ)
                    act.wait_ge(var_set, rnd + q + 1)
                    nc.scalar.activation(rstd[:, gs], rstd[:, gs], ACT.Sqrt).then_inc(std_set, 1)
                norms[0] += 1

            norms = [0]

            def dense(l, node):
                with act.Fori(0, STEPS) as n:
                    t = n + l * STEPS
                    act.wait_ge(dense_out, t + 1)
                    nc.scalar.activation(both[:, 0, :, 0:D], node[:, bass.ds(n * DB, DB), :], ACT.Copy).then_inc(catx_ready, 1)
                    act.wait_ge(cat_T, t + 1)
                    nc.scalar.activation(bothT[:, 0, :], stage[0][:, :], ACT.Copy).then_inc(catT_ready, 1)
                    if l == 0:
                        act.wait_ge(dense_done, t + 1)
                        nc.scalar.activation(total[:, bass.ds(n * DB, DB), :],
                                             stage[1][:, 0:DB * D].rearrange("p (g d) -> p g d", g=DB), ACT.Relu).then_inc(dense_out, 1)

            with act.Fori(0, LIGHT) as l:
                index_layer(l)
                clear(l, (l + 1) % 2)
            norm()
            act.wait_ge(unweighted, 1)
            index_layer(LIGHT)
            clear(LIGHT, 0)
            act.wait_ge(std_set, Q)
            dense(0, base)
            index_layer(LIGHT + 1)
            act.wait_ge(layer_done, LAYERS)
            dense(1, total)
            norm()

        @block.vector
        def _(dve):
            chained = [0]

            def link(ins):
                chained[0] += 1
                ins.then_inc(dve_chain, 1)
                dve.wait_ge(dve_chain, chained[0])

            link(nc.vector.memset(msg[:, :, D:D + 1], 1.0))
            link(nc.vector.memset(ones[:, :], 1.0))
            link(nc.vector.memset(zero[:, :], 0.0))
            link(nc.vector.memset(degree[:, :], 0.0))
            link(nc.vector.memset(zeros_b[:, :], 0.0))
            link(nc.vector.memset(count[:, :], 0.0))
            nc.vector.memset(item_at[:, 0:1], 0.0).then_inc(slot_free, RING)
            nc.vector.memset(count[0:COUNT_P, NB:NB + 1], float(COUNT_F)).then_inc(bank_free, BANKS)
            dve.wait_ge(bank_free, BANKS)
            dve.wait_ge(slot_free, RING)
            dve.wait_ge(iota_set, 1)
            link(nc.vector.tensor_copy(iota_p[:, :], iota_i[:, :]))
            dve.wait_ge(s_dst, 16)
            link(nc.vector.tensor_copy(dst_f, dst_i))
            for b in range(1, NB):
                link(nc.vector.tensor_scalar(below, dst_f, float(BN * b), None, ALU.is_lt, ALU.add,
                                             accum_out=count[0:COUNT_P, b:b + 1]))
            nc.vector.memset(shift[:, :], 0.0).then_inc(counted, 1)
            dve.wait_ge(edge_sum, 1)
            link(nc.vector.tensor_copy(edge_at[:, :], stage[0][:, 0:NB + 1]))
            link(nc.vector.tensor_copy(edge_i[:, :], edge_at[:, :]))
            link(nc.vector.tensor_scalar(row_i[:, :], edge_i[:, :], 7, None, ALU.arith_shift_right))
            link(nc.vector.tensor_copy(row_at[:, :], row_i[:, :]))
            link(nc.vector.tensor_scalar(last_f[:, :], edge_at[:, 1:NB + 1], -1.0, None, ALU.add))
            link(nc.vector.tensor_copy(last_i[:, :], last_f[:, :]))
            link(nc.vector.tensor_scalar(last_i[:, :], last_i[:, :], 7, None, ALU.arith_shift_right))
            link(nc.vector.tensor_copy(last_f[:, :], last_i[:, :]))
            link(nc.vector.tensor_tensor(some[:, :], edge_at[:, 1:NB + 1], edge_at[:, 0:NB], ALU.is_gt))
            link(nc.vector.scalar_tensor_tensor(rows_of[:, :], last_f[:, :], 1.0, row_at[:, 0:NB], ALU.add, ALU.subtract))
            link(nc.vector.tensor_tensor(rows_of[:, :], rows_of[:, :], some[:, :], ALU.mult))
            link(nc.vector.tensor_tensor_scan(item_at[:, 1:NB + 1], rows_of[:, :], zeros_b[:, :], 0.0, ALU.add, ALU.add))
            link(nc.vector.tensor_tensor(lag[:, :], row_at[:, 0:NB], item_at[:, 0:NB], ALU.subtract))
            link(nc.vector.tensor_tensor(slip[:, :], lag[:, 1:NB], lag[:, 0:NB - 1], ALU.subtract))
            dve.wait_ge(item_set, 1)
            link(nc.vector.tensor_copy(item_f[:, :], item_i[:, :]))
            wide = [P, CHUNKS, NB - 1]
            link(nc.vector.tensor_tensor(begun[:, :, :], item_at[:, 1:NB].unsqueeze(1).to_broadcast(wide),
                                         item_f[:, :].unsqueeze(2).to_broadcast(wide), ALU.is_le))
            link(nc.vector.tensor_tensor(slips[:, :, :], begun[:, :, :], slip[:, :].unsqueeze(1).to_broadcast(wide), ALU.mult))
            link(nc.vector.tensor_reduce(block_f[:, :], begun[:, :, :], AX.X, ALU.add))
            link(nc.vector.tensor_reduce(shift[:, :], slips[:, :, :], AX.X, ALU.add))
            link(nc.vector.tensor_tensor(row_of[:, :], item_f[:, :], shift[:, :], ALU.add))
            link(nc.vector.tensor_scalar(first_dst[:, :], block_f[:, :], float(BN), None, ALU.mult))
            nc.vector.tensor_scalar(first_grp[:, :], block_f[:, :], float(SB), None, ALU.mult).then_inc(grp_ready, 1)
            nc.vector.memset(zeros_b[:, :], 0.0).then_inc(rows_set, 1)
            nc.vector.memset(sum_f[:, :], 0.0).then_inc(tab_done, 2)
            with dve.Fori(0, CHUNKS // 2) as pair:
                for h in range(2):
                    k = pair * 2
                    dve.wait_ge(rows_in[h], pair * 16 + 16)
                    dve.wait_ge(tab_done, k + h + 1)
                    nc.vector.tensor_scalar(low[:, h, :], rows[:, h, 0, :], P - 1, None, ALU.bitwise_and).then_inc(s_low, 1)
                    nc.vector.tensor_scalar(high[:, h, :], rows[:, h, 0, :], 7, None, ALU.arith_shift_right).then_inc(s_low, 1)
                    nc.vector.tensor_scalar(rowf[:, h, 1, :], rows[:, h, 1, :], first_dst[:, bass.ds(k + h, 1)], None,
                                            ALU.subtract).then_inc(s_low, 1)
                    dve.wait_ge(s_low, (k + h + 1) * 3)
                    nc.vector.scalar_tensor_tensor(rowf[:, h, 0, :], low[:, h, :], float(G), high[:, h, :],
                                                   ALU.mult, ALU.add).then_inc(row_done, 1)
            dve.wait_ge(tab_done, 2 + CHUNKS)
            dve.wait_ge(grp_flat, 16)
            dve.wait_ge(s_total, 1)

            def one_hot(s, h, c):
                nc.vector.tensor_scalar(hot[:, s, :], iota_p[:, :], dst_c[:, h, c:c + 1], wgt_c[:, h, c:c + 1],
                                        ALU.is_equal, ALU.mult).then_inc(hot_ready, 1)

            def add_layer(layer, half, degrees):
                def body(turn, last):
                    i0 = turn * BODY
                    i = layer * ITEMS + i0
                    chunk = layer * (ITEMS // RING) + turn * 2
                    for h in range(2):
                        _, groups = nc.values_load_multi_w_load_instructions(
                            group_of[0:1, bass.ds(i0 + h * RING, RING)], engines=[mybir.EngineType.DVE], min_val=0, max_val=G - SB,
                            skip_runtime_bounds_check_because="a block's first group is below G by construction")
                        for jj in range(RING):
                            j = h * RING + jj
                            ahead = j + LOOKAHEAD
                            if j % 2 == 0:
                                if not (last and ahead >= BODY):
                                    if ahead % RING == 0:
                                        dve.wait_ge(cols_ready, chunk + (ahead // RING + 1))
                                    dve.wait_ge(slot_free, i + (ahead + 2 + RING - HOTS))
                                    for k in (ahead, ahead + 1):
                                        one_hot(k % HOTS, k // RING % 2, k % RING)
                                dve.wait_ge(slot_free, i + (RING + j + 2))
                            dve.wait_ge(bank_free, i + (BANKS + j))
                            if degrees:
                                d = degree[:, bass.ds(groups[jj], SB)]
                                nc.vector.tensor_tensor(d, d, sums[j % BANKS][:, :, D], ALU.add).then_inc(deg_added, 1)
                            a = (agg[:, half, bass.ds(groups[jj], SB), :] if isinstance(half, int) else
                                 agg[:, bass.ds(half, 1), bass.ds(groups[jj], SB), :].rearrange("p l g d -> p (l g) d"))
                            nc.vector.tensor_tensor(a, a, sums[j % BANKS][:, :, 0:D], ALU.add).then_inc(bank_free, 1)

                dve.wait_ge(cols_ready, layer * (ITEMS // RING) + 1)
                for k in range(LOOKAHEAD):
                    one_hot(k, 0, k)
                with dve.Fori(0, ITEMS // BODY - 1) as turn:
                    body(turn, False)
                body(ITEMS // BODY - 1, True)

            with dve.Fori(0, LIGHT) as l:
                dve.wait_ge(agg_zero, l + 2)
                add_layer(l, l % 2, False)
                dve.wait_ge(bank_free, (l + 1) * ITEMS + BANKS)
                nc.vector.memset(sum_f[:, :], 0.0).then_inc(layer_done, 1)
                half = agg[:, bass.ds(l % 2, 1), :, :].rearrange("p l g d -> p (l g) d")
                nc.vector.tensor_tensor(total[:, :, :], total[:, :, :], half, ALU.add).then_inc(summed, 1)
                dve.wait_ge(summed, l + 1)

            def norm(n):
                def wide(v):
                    return v.unsqueeze(2).to_broadcast([P, GQ, D])
                for q in range(Q):
                    gs = slice(q * GQ, (q + 1) * GQ)
                    link(nc.vector.tensor_reduce(sum_f[:, gs], base[:, gs, :], AX.X, ALU.add))
                    link(nc.vector.tensor_scalar(stage[2][:, gs], sum_f[:, gs], 1.0 / D, None, ALU.mult))
                    nc.vector.tensor_tensor(base[:, gs, :], base[:, gs, :], wide(stage[2][:, gs]), ALU.subtract).then_inc(centred, 1)
                for q in range(Q):
                    gs = slice(q * GQ, (q + 1) * GQ)
                    dve.wait_ge(squared, n * Q + q + 1)
                    link(nc.vector.tensor_reduce(sum_f[:, gs], total[:, gs, :], AX.X, ALU.add))
                    nc.vector.tensor_scalar(rstd[:, gs], sum_f[:, gs], 1.0 / D, EPS, ALU.mult, ALU.add).then_inc(var_set, 1)
                for q in range(Q):
                    gs = slice(q * GQ, (q + 1) * GQ)
                    dve.wait_ge(std_set, n * Q + q + 1)
                    link(nc.vector.reciprocal(stage[2][:, gs], rstd[:, gs]))
                    nc.vector.tensor_tensor(base[:, gs, :], base[:, gs, :], wide(stage[2][:, gs]), ALU.mult).then_inc(normed, 1)

            dve.wait_ge(cols_ready, LIGHT * (ITEMS // RING))
            nc.vector.memset(wgt_t[:, :], 1.0).then_inc(unweighted, 1)
            link(nc.vector.scalar_tensor_tensor(base[:, :, :].rearrange("p g d -> p (g d)"), total[:, :, :].rearrange("p g d -> p (g d)"),
                                                1.0 / (LIGHT + 1), base[:, :, :].rearrange("p g d -> p (g d)"), ALU.mult, ALU.add))
            norm(0)
            dve.wait_ge(agg_zero, LIGHT + 2)
            add_layer(LIGHT, 1, True)
            dve.wait_ge(bank_free, (LIGHT + 1) * ITEMS + BANKS)
            dve.wait_ge(deg_added, ITEMS)
            nc.vector.memset(sum_f[:, :], 0.0).then_inc(layer_done, 1)
            link(nc.vector.tensor_scalar(rdeg[:, :], degree[:, :], 1.0, None, ALU.max))
            link(nc.vector.reciprocal(rdeg[:, :], rdeg[:, :]))
            link(nc.vector.tensor_copy(stage[2][:, 0:G], rdeg[:, :]))

            def mean(l, n, half):
                dve.wait_ge(dense_out, n + (l * STEPS + 1))
                gs = bass.ds(n * DB, DB)
                nc.vector.tensor_tensor(both[:, 0, :, D:2 * D], agg[:, half, gs, :],
                                        stage[2][:, gs].unsqueeze(2).to_broadcast([P, DB, D]), ALU.mult).then_inc(cat_ready, 1)

            nc.vector.memset(zeros_b[:, :], 0.0).then_inc(dense_out, 1)
            with dve.Fori(0, STEPS) as n:
                mean(0, n, 1)
            dve.wait_ge(agg_zero, LIGHT + 3)
            add_layer(LIGHT + 1, 0, False)
            dve.wait_ge(bank_free, LAYERS * ITEMS + BANKS)
            nc.vector.memset(sum_f[:, :], 0.0).then_inc(layer_done, 1)
            with dve.Fori(0, STEPS) as n:
                mean(1, n, 0)
                dve.wait_ge(dense_done, n + (STEPS + 1))
                gs = bass.ds(n * DB, DB)
                nc.vector.tensor_tensor(base[:, gs, :], base[:, gs, :],
                                        stage[1][:, 0:DB * D].rearrange("p (g d) -> p g d", g=DB), ALU.add).then_inc(dense_out, 1)
            dve.wait_ge(dense_out, 2 * STEPS + 1)
            norm(1)


ARGS = ["x", "src", "dst", "edge_weight", "L1_gnn_W_self1", "L1_gnn_W_neigh1", "L1_gnn_b1",
        "L1_gnn_W_self2", "L1_gnn_W_neigh2", "L1_gnn_b2"]


def kernel(**inputs):
    import concourse.bacc as bacc
    from concourse.bass_utils import run_bass_kernel_spmd

    nc = bacc.Bacc("TRN2", target_bir_lowering=False, num_devices=1)
    arrays, args = {}, []
    for name in ARGS:
        a = np.ascontiguousarray(inputs[name])
        arrays[f"in_{name}"] = a
        args.append(nc.dram_tensor(f"in_{name}", a.shape, mybir.dt.from_np(a.dtype), kind="ExternalInput").ap())
    args.append(nc.dram_tensor("out", (N, D), F32, kind="ExternalOutput").ap())
    build_program(nc, *args)
    result = run_bass_kernel_spmd(nc, [arrays], core_ids=[0])
    return result.results[0]["out"]
```

```python
from contextlib import ExitStack

import numpy as np

import concourse.bass as bass
from concourse import mybir

F32 = mybir.dt.float32
I32 = mybir.dt.int32
U16 = mybir.dt.uint16
ALU = mybir.AluOpType
ACT = mybir.ActivationFunctionType
AX = mybir.AxisListType

P = 128
N, D, E = 15625, 64, 250000
LIGHT, SAGE = 3, 2
LAYERS = LIGHT + SAGE
EPS = 1e-5

SB = 2
BN = SB * P
NB = -(-N // BN)
G = NB * SB
WHOLE = N // P
NPAD = G * P
ROWS = -(-E // P)
FULL = E // P
LAST = E - FULL * P
CH = 16
BODY = 2 * CH
ITEMS = -(-(ROWS + NB - 1) // BODY) * BODY
RCH = -(-ROWS // CH)
SETS = -(-ITEMS // P)
SLOTS = SETS * P
RING = P
SEMS = 2 * CH
HOTS = 8
LOOKAHEAD = 4
BANKS = 4
COUNT_P, COUNT_F = 125, E // 125
NOWHERE = 1 << 20
DB = 4
STEPS = G // DB
Q = 4
PART = [0, 32, 64, 96, G]
assert RCH % 2 == 1 and STEPS % 2 == 1 and ROWS % SEMS == 2 and RING >= NB + 4 * CH
XNODES = 3
TOTAL = 2


def build_program(nc, x, src, dst, edge_weight, w_self1, w_neigh1, b1, w_self2, w_neigh2, b2, out):
    table = [nc.dram_tensor(f"table{l}", (NPAD, D), F32, kind="Internal").ap() for l in range(LAYERS)]
    table_p = [t.rearrange("(p g) d -> p g d", p=P) for t in table]
    edges = nc.dram_tensor("edges", (SLOTS, 3 * P), I32, kind="Internal").ap()
    edges3 = edges.rearrange("r (a e) -> r a e", a=3)

    ctx = ExitStack()
    with ctx:
        def sb(name, shape, dt=F32):
            return ctx.enter_context(nc.sbuf_tensor(name, shape, dt))

        def ps(name, shape, dt=F32):
            return ctx.enter_context(nc.psum_tensor(name, shape, dt))

        def sem(name):
            return ctx.enter_context(nc.semaphore(name))

        nodes = sb("nodes", [P, 4, G, D])
        degree = sb("degree", [P, G])
        src_t = sb("src_t", [P, SLOTS], U16)
        edge_t = sb("edge_t", [P, SLOTS, 2])
        item_regs = sb("item_regs", [3, SLOTS], U16)
        index = sb("index", [P, 2, CH], I32)
        edge_c = sb("edge_c", [P, 2, CH, 2])
        msg = sb("msg", [P, RING, D + 1])
        hot = sb("hot", [P, HOTS, BN])
        ident = sb("ident", [P, P])
        ones = sb("ones", [P, P])
        zero = sb("zero", [P, 1])
        weights = sb("weights", [P, 2, D])
        bias = sb("bias", [1, 2, DB, D])
        count = sb("count", [P, NB + 1])
        edge_at = sb("edge_at", [P, NB + 1])
        edge_i = sb("edge_i", [P, NB + 1], I32)
        row_i = sb("row_i", [P, NB + 1], I32)
        row_at = sb("row_at", [P, NB + 1])
        last_f = sb("last_f", [P, NB])
        last_i = sb("last_i", [P, NB], I32)
        some = sb("some", [P, NB])
        rows_of = sb("rows_of", [P, NB])
        item_at = sb("item_at", [P, NB + 1])
        item_at_i = sb("item_at_i", [1, NB + 1], I32)
        lag = sb("lag", [P, NB])
        slip = sb("slip", [P, NB - 1])
        zeros_b = sb("zeros_b", [P, NB])
        item_i = sb("item_i", [P, SETS], I32)
        item_f = sb("item_f", [P, SETS])
        block_f = sb("block_f", [P, SETS])
        first_dst = sb("first_dst", [P, SETS])
        shift = sb("shift", [P, SETS])
        row_f = sb("row_f", [P, SETS])
        row_of = sb("row_of", [P, SETS], I32)
        held_i = sb("held_i", [P, SETS], I32)
        regs_f = sb("regs_f", [P, 3, SETS])
        pick = sb("pick", [P, 2], I32)
        rstd = sb("rstd", [P, G])
        sum_f = sb("sum_f", [P, G])
        rdeg = sb("rdeg", [P, G])
        both = sb("both", [P, 2, DB, 2 * D])
        bothT = sb("bothT", [P, 2, DB * P])
        rows = both[:, :, :, :].rearrange("p h g d -> p (h g d)")[:, 0:6 * P].bitcast(I32).rearrange(
            "p (h a e) -> p h a e", h=2, a=3)
        rowf = bothT[:, 0, 0:2 * P].rearrange("p (h e) -> p h e", h=2)
        iota_i = bothT[:, 1, 0:BN].bitcast(I32)
        regs_i = bothT[0:3 * SETS, 1, BN:BN + P // 2].bitcast(U16)
        room = nodes[:, 1, :, :].rearrange("p g d -> p (g d)")
        dst_i = room[0:COUNT_P, 0:COUNT_F].bitcast(I32)
        dst_f = room[0:COUNT_P, COUNT_F:2 * COUNT_F]
        below = room[0:COUNT_P, 2 * COUNT_F:3 * COUNT_F]
        tail = room[0:SLOTS - FULL, 3 * COUNT_F:3 * COUNT_F + 3 * P].bitcast(I32).rearrange("p (a e) -> p a e", a=3)
        begun = room[:, 3 * COUNT_F + 3 * P:3 * COUNT_F + 3 * P + SETS * (NB - 1)].rearrange("p (k b) -> p k b", k=SETS)
        slips = room[:, 0:SETS * (NB - 1)].rearrange("p (k b) -> p k b", k=SETS)
        src_rows, low, high = (nodes[:, 0, :, :].rearrange("p g d -> p (g d)")[:, n * SLOTS:(n + 1) * SLOTS].bitcast(I32)
                               for n in range(3))

        iota_p = ps("iota_p", [P, BN])
        sums = [ps(f"sums{i}", [P, 512]) for i in range(BANKS)]
        stage = [ps(f"stage{i}", [P, 512]) for i in range(3)]

        x_in, dst_in, par_in, tail_in, edges_out, src_in = (
            sem(n) for n in ("x_in", "dst_in", "par_in", "tail_in", "edges_out", "src_in"))
        pads_set, tail_set, iota_set, item_set, ident_set = (
            sem(n) for n in ("pads_set", "tail_set", "iota_set", "item_set", "ident_set"))
        dve_chain = sem("dve_chain")
        src_split, src_done, src_T, src_tab = (sem(n) for n in ("src_split", "src_done", "src_T", "src_tab"))
        counted, edge_sum, rows_set, regs_ready, regs_T, regs_copied, regs_in = (
            sem(n) for n in ("counted", "edge_sum", "rows_set", "regs_ready", "regs_T", "regs_copied", "regs_in"))
        picked, row_done, row_T = sem("picked"), sem("row_done"), sem("row_T")
        rows_in = [sem(f"rows_in{h}") for h in range(2)]
        tab_done = sem("tab_done")
        total_set = sem("total_set")
        cleared = sem("cleared")
        layer_in = sem("layer_in")
        idx_ready = sem("idx_ready")
        landed = [sem(f"landed{j}") for j in range(SEMS)]
        rows_landed = sem("rows_landed")
        cols_in = sem("cols_in")
        hot_ready = sem("hot_ready")
        items_done = sem("items_done")
        bank_free = sem("bank_free")
        deg_added, summed = sem("deg_added"), sem("summed")
        paced = sem("paced")
        centred, squared, var_set, std_set, normed = (sem(n) for n in ("centred", "squared", "var_set", "std_set", "normed"))
        mean_ready, node_ready, catT_ready = sem("mean_ready"), sem("node_ready"), sem("catT_ready")
        cat_T = sem("cat_T")
        dense_done, dense_out = sem("dense_done"), sem("dense_out")
        out_done = sem("out_done")
        block = ctx.enter_context(nc.Block())

        def steps(eng, body):
            with eng.Fori(0, STEPS // 2) as two:
                body(two * 2, 0)
                body(two * 2 + 1, 1)
            body(STEPS - 1, 0)

        @block.sync
        def _(sp):
            lists = (src, dst, edge_weight.bitcast(I32))
            sp.dma_start(dst_i, dst.rearrange("(p f) -> p f", p=COUNT_P)).then_inc(dst_in, 16)
            for a, arr in enumerate(lists):
                sp.dma_start(edges3[0:FULL, a, :], arr[0:FULL * P].rearrange("(r e) -> r e", e=P)).then_inc(edges_out, 16)
            sp.wait_ge(tail_set, 3)
            for a, arr in enumerate(lists):
                sp.dma_start(tail[0:1, a, 0:LAST], arr[FULL * P:E].rearrange("(r e) -> r e", r=1)).then_inc(tail_in, 16)
            sp.wait_ge(tail_in, 48)
            sp.dma_start(edges3[FULL:SLOTS, :, :], tail).then_inc(edges_out, 16)
            sp.wait_ge(edges_out, 64)
            sp.dma_start(src_rows.rearrange("p (k e) -> p k e", k=SETS),
                         edges.rearrange("(k p) f -> p k f", p=P)[:, :, 0:P]).then_inc(src_in, 16)
            for l, (ws, wn, b) in enumerate(((w_self1, w_neigh1, b1), (w_self2, w_neigh2, b2))):
                sp.dma_start(weights[0:D, l, :], ws).then_inc(par_in, 16)
                sp.dma_start(weights[D:2 * D, l, :], wn).then_inc(par_in, 16)
                for g in range(DB):
                    sp.dma_start(bias[:, l, g, :], b.rearrange("(r d) -> r d", r=1)).then_inc(par_in, 16)

            def relay(layer):
                def row(j, use):
                    sp.wait_ge(landed[j], use * 16)
                    sp.sem_inc(rows_landed, 1)
                uses = [len(range(j, ROWS, SEMS)) for j in range(SEMS)]
                with sp.Fori(0, ROWS // SEMS) as turn:
                    for j in range(SEMS):
                        row(j, turn + (layer * uses[j] + 1))
                for j in range(ROWS % SEMS):
                    row(j, (layer + 1) * uses[j])

            for l in range(LAYERS):
                relay(l)
                for q in range(Q):
                    if l == LIGHT - 1:
                        sp.wait_ge(normed, q + 1)
                        sp.dma_start(table_p[LIGHT][:, PART[q]:PART[q + 1], :],
                                     nodes[:, TOTAL, PART[q]:PART[q + 1], :]).then_inc(layer_in, 16)
                    if l == LIGHT:
                        sp.wait_ge(dense_out, 2 + PART[q + 1] // DB)
                        sp.dma_start(table_p[LIGHT + 1][:, PART[q]:PART[q + 1], :],
                                     nodes[:, XNODES, PART[q]:PART[q + 1], :]).then_inc(layer_in, 16)
                    if l == LIGHT + 1:
                        sp.wait_ge(normed, Q + q + 1)
                        g0, g1 = PART[q], min(PART[q + 1], WHOLE)
                        sp.dma_start(out[g0 * P:g1 * P, :].rearrange("(g p) d -> p g d", p=P),
                                     nodes[:, TOTAL, g0:g1, :]).then_inc(out_done, 16)
            sp.dma_start(out[WHOLE * P:N, :], nodes[0:N - WHOLE * P, TOTAL, WHOLE, :]).then_inc(out_done, 16)
            sp.wait_ge(out_done, 16 * (Q + 1))
            sp.wait_ge(layer_in, 16 * Q * LAYERS)

        @block.gpsimd
        def _(pool):
            pool.memset(nodes[:, XNODES, WHOLE:G, :], 0.0).then_inc(pads_set, 1)
            for a, fill in enumerate((0, NOWHERE, 0)):
                pool.memset(tail[:, a, :], fill).then_inc(tail_set, 1)
            pool.iota(iota_i, [[1, BN]], base=0, channel_multiplier=0).then_inc(iota_set, 1)
            pool.memset(ident[:, :], 0.0).then_inc(ident_set, 1)
            pool.wait_ge(ident_set, 1)
            pool.affine_select(out=ident[:, :], in_=ident[:, :], compare_op=ALU.not_equal, fill=1.0, base=0,
                               pattern=[[-1, P]], channel_multiplier=1).then_inc(ident_set, 1)
            pool.iota(item_i[:, :], [[P, SETS]], base=0, channel_multiplier=1).then_inc(item_set, 1)

            def gather_chunk(layer, c, q, first):
                pool.wait_ge(idx_ready, c + (layer * RCH + 1))
                if not first:
                    pool.wait_ge(items_done, c * CH + (layer * ITEMS + CH - RING + NB + HOTS))
                    pool.sem_inc(paced, 1)
                for j in range(CH if not isinstance(c, int) else min(CH, ROWS - c * CH)):
                    pool.indirect_dma_start(msg[:, q * CH + j, 0:D], None, table[layer],
                                            bass.IndirectOffsetOnAxis(index[:, q % 2, j:j + 1], axis=0)
                                            ).then_inc(landed[q % 2 * CH + j], 16)

            per = RING // CH
            for l in range(LAYERS):
                pool.wait_ge(layer_in, (l + 1) * Q * 16)
                for q in range(per):
                    gather_chunk(l, q, q, True)
                if l == 0:
                    pool.wait_ge(edges_out, 64)
                    pool.wait_ge(rows_set, 1)
                    with pool.Fori(0, SETS // 2) as pair:
                        for h in range(2):
                            pool.wait_ge(tab_done, pair * 2 + (h + 1))
                            pool.tensor_copy(pick[:, h:h + 1], row_of[:, bass.ds(pair * 2 + h, 1)]).then_inc(picked, 1)
                            pool.wait_ge(picked, pair * 2 + (h + 1))
                            pool.sem_inc(paced, 1)
                            pool.indirect_dma_start(rows[:, h, :, :].rearrange("p a e -> p (a e)"), None, edges,
                                                    bass.IndirectOffsetOnAxis(pick[:, h:h + 1], axis=0)).then_inc(rows_in[h], 16)
                with pool.Fori(1, RCH // per) as turn:
                    for q in range(per):
                        gather_chunk(l, turn * per + q, q, False)
                for c in range(RCH // per * per, RCH):
                    gather_chunk(l, c, c % per, False)
                if l >= LIGHT:
                    src_of = TOTAL if l == LIGHT else XNODES

                    def copy(n, h):
                        pool.wait_ge(cat_T, n + ((l - LIGHT) * STEPS + 1))
                        pool.tensor_copy(both[:, h, :, 0:D], nodes[:, src_of, bass.ds(n * DB, DB), :]).then_inc(node_ready, 1)
                    steps(pool, copy)

        @block.tensor
        def _(pe):
            pe.wait_ge(ident_set, 2)
            pe.wait_ge(src_done, 1)
            src_f = high.bitcast(F32)
            for four in range(SETS // 4):
                if four >= 2:
                    pe.wait_ge(src_tab, four - 1)
                for k in range(4):
                    c = (four * 4 + k) * P
                    tr = nc.tensor.transpose(stage[four % 2][:, k * P:(k + 1) * P], src_f[:, c:c + P], ident[:, :])
                tr.then_inc(src_T, 1)
            pe.wait_ge(counted, 1)
            nc.tensor.matmul(stage[2][:, 0:NB + 1], ones[:, :], count[:, :], start=True, stop=True).then_inc(edge_sum, 1)
            pe.wait_ge(regs_ready, 1)
            nc.tensor.transpose(stage[2][0:3 * SETS, 0:P], regs_f[:, :, :].rearrange("p a k -> p (a k)"), ident[:, :]).then_inc(regs_T, 1)
            pe.wait_ge(src_tab, SETS // 4)
            with pe.Fori(0, SETS // 2) as pair:
                for h in range(2):
                    pe.wait_ge(row_done, pair * 2 + (h + 1))
                    pe.wait_ge(tab_done, pair * 2 + (h + 1))
                    nc.tensor.transpose(stage[h][:, 0:P], rowf[:, h, :], ident[:, :])
                    nc.tensor.transpose(stage[h][:, P:2 * P], rows[:, h, 2, :].bitcast(F32), ident[:, :]).then_inc(row_T, 1)
            pe.wait_ge(regs_in, 48)
            flat = msg[:, :, :].rearrange("p r d -> p (r d)")

            def slots(at):
                return nc.values_load_multi_w_load_instructions(
                    item_regs[1:2, bass.ds(at, CH)], engines=[mybir.EngineType.PE], min_val=0, max_val=(RING - 1) * (D + 1),
                    skip_runtime_bounds_check_because="a slot is a row's low bits")[1]

            def rows_needed(at):
                return nc.values_load_multi_w_load_instructions(
                    item_regs[2:3, bass.ds(at + 3, CH // 4, 4)], engines=[mybir.EngineType.PE], min_val=1, max_val=ROWS)[1]

            def sum_layer(layer, width):
                with pe.Fori(0, ITEMS // BODY) as turn:
                    i = turn * BODY + layer * ITEMS
                    for h in range(2):
                        at = slots(turn * BODY + h * CH)
                        need = rows_needed(turn * BODY + h * CH)
                        for jj in range(CH):
                            j = h * CH + jj
                            if j % 4 == 0:
                                pe.wait_ge(rows_landed, need[jj // 4] + layer * ROWS)
                            if j % 2 == 0:
                                pe.wait_ge(bank_free, i + (j + 2))
                                pe.wait_ge(hot_ready, i + (j + 2))
                            for g in range(SB):
                                mm = nc.tensor.matmul(sums[j % BANKS][:, g * width:(g + 1) * width],
                                                      hot[:, j % HOTS, g * P:(g + 1) * P],
                                                      flat[:, bass.ds(at[jj], width)], start=True, stop=True)
                            mm.then_inc(items_done, 1)

            def dense(l):
                def turn_over(n, h):
                    t = n + l * STEPS
                    pe.wait_ge(mean_ready, t + 1)
                    pe.wait_ge(node_ready, t + 1)
                    pe.wait_ge(catT_ready, t + 1)
                    for g in range(DB):
                        tr = nc.tensor.transpose(stage[h][:, g * P:(g + 1) * P], both[:, h, g, :], ident[:, :])
                    tr.then_inc(cat_T, 1)

                def product(n, h):
                    t = n + l * STEPS
                    pe.wait_ge(catT_ready, t + 3)
                    pe.wait_ge(dense_out, t + 1)
                    for g in range(DB):
                        o = sums[h][:, g * D:(g + 1) * D]
                        nc.tensor.matmul(o, bothT[:, h, g * P:(g + 1) * P], weights[:, l, :], start=True, stop=False)
                        if l == 1:
                            nc.tensor.matmul(o, ident[:, :], nodes[:, TOTAL, bass.ds(n * DB + g, 1), :].rearrange("p g d -> p (g d)"),
                                             start=False, stop=False)
                        mm = nc.tensor.matmul(o, ones[0:1, :], bias[:, l, g, :], start=False, stop=True)
                    mm.then_inc(dense_done, 1)

                turn_over(0, 0)
                with pe.Fori(0, STEPS // 2) as two:
                    turn_over(two * 2 + 1, 1)
                    product(two * 2, 0)
                    turn_over(two * 2 + 2, 0)
                    product(two * 2 + 1, 1)
                product(STEPS - 1, 0)

            with pe.Fori(0, LIGHT) as l:
                sum_layer(l, D)
            sum_layer(LIGHT, D + 1)
            pe.wait_ge(par_in, 16 * 2 * (2 + DB))
            dense(0)
            sum_layer(LIGHT + 1, D)
            dense(1)

        @block.scalar
        def _(act):
            act.dma_start(nodes[:, XNODES, 0:WHOLE, :], x[0:WHOLE * P, :].rearrange("(g p) d -> p g d", p=P)).then_inc(x_in, 16)
            act.wait_ge(pads_set, 1)
            act.dma_start(nodes[0:N - WHOLE * P, XNODES, WHOLE, :], x[WHOLE * P:N, :]).then_inc(x_in, 16)
            act.wait_ge(x_in, 32)
            for q in range(Q):
                act.dma_start(table_p[0][:, PART[q]:PART[q + 1], :], nodes[:, XNODES, PART[q]:PART[q + 1], :]).then_inc(layer_in, 16)
            for four in range(SETS // 4):
                act.wait_ge(src_T, four + 1)
                nc.scalar.activation(src_t[:, four * 512:(four + 1) * 512], stage[four % 2][:, :], ACT.Copy).then_inc(src_tab, 1)
            act.wait_ge(src_tab, SETS // 4)

            def node_row(n):
                return nodes[:, n, :, :].rearrange("p g d -> p (g d)")

            def clear(n):
                nc.scalar.activation(node_row(n), zero[:, 0:1].to_broadcast([P, G * D]), ACT.Copy).then_inc(cleared, 1)

            def index_chunks(layer, some):
                def chunk(c, h):
                    act.wait_ge(rows_landed, c * CH + (layer * ROWS - CH + 1))
                    nc.scalar.activation(index[:, h, :], src_t[:, bass.ds(c * CH, CH)], ACT.Copy).then_inc(idx_ready, 1)
                if some[0] == 0:
                    if layer:
                        act.wait_ge(rows_landed, layer * ROWS)
                    nc.scalar.activation(index[:, 0, :], src_t[:, 0:CH], ACT.Copy).then_inc(idx_ready, 1)
                with act.Fori(some[0] // 2, some[1] // 2) as two:
                    chunk(two * 2 + 1, 1)
                    chunk(two * 2 + 2, 0)

            index_chunks(0, (0, RING // CH))
            nc.scalar.activation(node_row(TOTAL), node_row(XNODES), ACT.Copy, scale=float(LIGHT + 2)).then_inc(total_set, 1)
            clear(0)
            act.wait_ge(regs_T, 1)
            nc.scalar.activation(regs_i, stage[2][0:3 * SETS, 0:P], ACT.Copy).then_inc(regs_copied, 1)
            act.wait_ge(regs_copied, 1)
            for n in range(3):
                act.dma_start(item_regs[n:n + 1, :].rearrange("r (k p) -> r k p", k=SETS),
                             regs_i[n * SETS:(n + 1) * SETS, :]).then_inc(regs_in, 16)
            with act.Fori(0, SETS // 2) as pair:
                for h in range(2):
                    act.wait_ge(row_T, pair * 2 + (h + 1))
                    nc.scalar.activation(edge_t[:, bass.ds((pair * 2 + h) * P, P), :].rearrange("p c a -> p a c"),
                                         stage[h][:, 0:2 * P].rearrange("p (a c) -> p a c", a=2), ACT.Copy).then_inc(tab_done, 1)

            def norm(n, squares, scale):
                for q in range(Q):
                    gs = slice(PART[q], PART[q + 1])
                    act.wait_ge(centred, n * Q + q + 1)
                    nc.scalar.activation(nodes[:, squares, gs, :], nodes[:, TOTAL, gs, :], ACT.Square).then_inc(squared, 1)
                for q in range(Q):
                    gs = slice(PART[q], PART[q + 1])
                    act.wait_ge(var_set, n * Q + q + 1)
                    nc.scalar.activation(rstd[:, gs], rstd[:, gs], ACT.Sqrt, scale=scale).then_inc(std_set, 1)

            def dense(l, to, func):
                def columns(n, h):
                    t = n + l * STEPS
                    act.wait_ge(cat_T, t + 3)
                    nc.scalar.activation(bothT[:, h, :], stage[h][:, :], ACT.Copy).then_inc(catT_ready, 1)

                def result(n, h):
                    act.wait_ge(dense_done, n + (l * STEPS + 1))
                    nc.scalar.activation(nodes[:, to, bass.ds(n * DB, DB), :],
                                         sums[h][:, 0:DB * D].rearrange("p (g d) -> p g d", g=DB), func).then_inc(dense_out, 1)

                columns(0, 0)
                with act.Fori(0, STEPS // 2) as two:
                    columns(two * 2 + 1, 1)
                    result(two * 2, 0)
                    columns(two * 2 + 2, 0)
                    result(two * 2 + 1, 1)
                result(STEPS - 1, 0)

            for l in range(LAYERS):
                index_chunks(l, (RING // CH if l == 0 else 0, RCH))
                if l == 0:
                    act.wait_ge(tab_done, 2 + SETS)
                    clear(1)
                if l in (1, 2):
                    act.wait_ge(summed, l)
                    clear(l - 1)
                if l < LIGHT - 1:
                    for q in range(Q):
                        if q < Q - 1:
                            upto = act.value_load(item_at_i[0:1, PART[q + 1] // SB:PART[q + 1] // SB + 1], min_val=0, max_val=ITEMS)
                            act.wait_ge(bank_free, upto + (l * ITEMS + BANKS))
                        else:
                            act.wait_ge(bank_free, (l + 1) * ITEMS + BANKS)
                        act.dma_start(table_p[l + 1][:, PART[q]:PART[q + 1], :],
                                      nodes[:, l, PART[q]:PART[q + 1], :]).then_inc(layer_in, 16)
                if l == LIGHT - 1:
                    norm(0, XNODES, float((LIGHT + 1) ** 2))
                if l == LIGHT:
                    dense(0, XNODES, ACT.Relu)
                if l == LIGHT + 1:
                    dense(1, TOTAL, ACT.Copy)
                    norm(1, 0, 1.0)

        @block.vector
        def _(dve):
            chained = [0]

            def link(ins):
                chained[0] += 1
                ins.then_inc(dve_chain, 1)
                dve.wait_ge(dve_chain, chained[0])

            nc.vector.memset(ones[:, :], 1.0)
            nc.vector.memset(zero[:, :], 0.0)
            nc.vector.memset(degree[:, :], 0.0)
            nc.vector.memset(zeros_b[:, :], 0.0)
            nc.vector.memset(item_at[:, 0:1], 0.0)
            nc.vector.memset(msg[:, :, D:D + 1], 1.0)
            link(nc.vector.memset(count[:, :], 0.0))
            link(nc.vector.memset(count[0:COUNT_P, NB:NB + 1], float(COUNT_F)))
            dve.sem_inc(items_done, HOTS)
            dve.sem_inc(bank_free, BANKS)
            for ready in (tab_done, cat_T, catT_ready, dense_out):
                dve.sem_inc(ready, 2)
            dve.wait_ge(src_in, 16)
            nc.vector.tensor_scalar(low, src_rows, P - 1, None, ALU.bitwise_and).then_inc(src_split, 1)
            nc.vector.tensor_scalar(high, src_rows, 7, None, ALU.arith_shift_right).then_inc(src_split, 1)
            dve.wait_ge(src_split, 2)
            nc.vector.scalar_tensor_tensor(high.bitcast(F32), low, float(G), high, ALU.mult, ALU.add).then_inc(src_done, 1)
            dve.wait_ge(dst_in, 16)
            link(nc.vector.tensor_copy(dst_f, dst_i))
            for b in range(1, NB):
                link(nc.vector.tensor_scalar(below, dst_f, float(BN * b), None, ALU.is_lt, ALU.add,
                                             accum_out=count[0:COUNT_P, b:b + 1]))
            dve.sem_inc(counted, 1)
            dve.wait_ge(iota_set, 1)
            nc.vector.tensor_copy(iota_p[:, :], iota_i)
            dve.wait_ge(edge_sum, 1)
            link(nc.vector.tensor_copy(edge_at[:, :], stage[2][:, 0:NB + 1]))
            link(nc.vector.tensor_copy(edge_i[:, :], edge_at[:, :]))
            link(nc.vector.tensor_scalar(row_i[:, :], edge_i[:, :], 7, None, ALU.arith_shift_right))
            link(nc.vector.tensor_copy(row_at[:, :], row_i[:, :]))
            link(nc.vector.tensor_scalar(last_f[:, :], edge_at[:, 1:NB + 1], -1.0, None, ALU.add))
            link(nc.vector.tensor_copy(last_i[:, :], last_f[:, :]))
            link(nc.vector.tensor_scalar(last_i[:, :], last_i[:, :], 7, None, ALU.arith_shift_right))
            link(nc.vector.tensor_copy(last_f[:, :], last_i[:, :]))
            link(nc.vector.tensor_tensor(some[:, :], edge_at[:, 1:NB + 1], edge_at[:, 0:NB], ALU.is_gt))
            link(nc.vector.scalar_tensor_tensor(rows_of[:, :], last_f[:, :], 1.0, row_at[:, 0:NB], ALU.add, ALU.subtract))
            link(nc.vector.tensor_tensor(rows_of[:, :], rows_of[:, :], some[:, :], ALU.mult))
            link(nc.vector.tensor_tensor_scan(item_at[:, 1:NB + 1], rows_of[:, :], zeros_b[:, :], 0.0, ALU.add, ALU.add))
            link(nc.vector.tensor_copy(item_at_i[:, :], item_at[0:1, :]))
            link(nc.vector.tensor_tensor(lag[:, :], row_at[:, 0:NB], item_at[:, 0:NB], ALU.subtract))
            link(nc.vector.tensor_tensor(slip[:, :], lag[:, 1:NB], lag[:, 0:NB - 1], ALU.subtract))
            dve.wait_ge(item_set, 1)
            link(nc.vector.tensor_copy(item_f[:, :], item_i[:, :]))
            wide = [P, SETS, NB - 1]
            link(nc.vector.tensor_tensor(begun, item_at[:, 1:NB].unsqueeze(1).to_broadcast(wide),
                                         item_f[:, :].unsqueeze(2).to_broadcast(wide), ALU.is_le))
            link(nc.vector.tensor_tensor(slips, begun, slip[:, :].unsqueeze(1).to_broadcast(wide), ALU.mult))
            link(nc.vector.tensor_reduce(block_f[:, :], begun, AX.X, ALU.add))
            link(nc.vector.tensor_reduce(shift[:, :], slips, AX.X, ALU.add))
            link(nc.vector.tensor_scalar(first_dst[:, :], block_f[:, :], float(BN), None, ALU.mult))
            link(nc.vector.tensor_tensor(row_f[:, :], item_f[:, :], shift[:, :], ALU.add))
            link(nc.vector.tensor_copy(row_of[:, :], row_f[:, :]))
            dve.sem_inc(rows_set, 1)
            link(nc.vector.tensor_scalar(regs_f[:, 0, :], block_f[:, :], float(SB), None, ALU.mult))
            link(nc.vector.tensor_scalar(row_f[:, :], row_f[:, :], float(ROWS - 1), None, ALU.min))
            link(nc.vector.tensor_scalar(regs_f[:, 2, :], row_f[:, :], 1.0, None, ALU.add))
            link(nc.vector.tensor_copy(held_i[:, :], row_f[:, :]))
            link(nc.vector.tensor_scalar(held_i[:, :], held_i[:, :], RING - 1, None, ALU.bitwise_and))
            nc.vector.tensor_scalar(regs_f[:, 1, :], held_i[:, :], float(D + 1), None, ALU.mult).then_inc(regs_ready, 1)
            with dve.Fori(0, SETS // 2) as pair:
                for h in range(2):
                    dve.wait_ge(rows_in[h], pair * 16 + 16)
                    dve.wait_ge(tab_done, pair * 2 + (h + 1))
                    nc.vector.tensor_scalar(rowf[:, h, :], rows[:, h, 1, :], first_dst[:, bass.ds(pair * 2 + h, 1)], None,
                                            ALU.subtract).then_inc(row_done, 1)
            dve.wait_ge(tab_done, 2 + SETS)
            dve.wait_ge(regs_in, 48)
            dve.wait_ge(total_set, 1)

            def columns(layer, at, chunk, h):
                nc.vector.tensor_copy(edge_c[:, h, :, :], edge_t[:, bass.ds(at, CH), :]).then_inc(cols_in, 1)
                dve.wait_ge(cols_in, chunk + (layer * (ITEMS // CH) + 1))

            def one_hot(j):
                c = edge_c[:, j // CH % 2, j % CH, :]
                nc.vector.tensor_scalar(hot[:, j % HOTS, :], iota_p[:, :], c[:, 0:1], c[:, 1:2],
                                        ALU.is_equal, ALU.mult).then_inc(hot_ready, 1)

            def add_layer(layer, to, degrees):
                width = D + 1 if degrees else D

                def body(turn, last):
                    i = turn * BODY + layer * ITEMS
                    for h in range(2):
                        groups = nc.values_load_multi_w_load_instructions(
                            item_regs[0:1, bass.ds(turn * BODY + h * CH, CH)], engines=[mybir.EngineType.DVE],
                            min_val=0, max_val=G - SB,
                            skip_runtime_bounds_check_because="a block's first group is below G by construction")[1]
                        for jj in range(CH):
                            j = h * CH + jj
                            ahead = j + LOOKAHEAD
                            if not (last and ahead >= BODY):
                                if ahead % CH == 0:
                                    columns(layer, turn * BODY + ahead, turn * 2 + ahead // CH, ahead // CH % 2)
                                if j % 2 == 0:
                                    dve.wait_ge(items_done, i + (ahead + 2))
                                one_hot(ahead)
                            if j % 2 == 0:
                                dve.wait_ge(items_done, i + (HOTS + j + 2))
                            dve.wait_ge(bank_free, i + (BANKS + j))
                            got = sums[j % BANKS][:, 0:SB * width].rearrange("p (g d) -> p g d", g=SB)
                            if degrees:
                                d = degree[:, bass.ds(groups[jj], SB)]
                                nc.vector.tensor_tensor(d, d, got[:, :, D], ALU.add).then_inc(deg_added, 1)
                            s = (nodes[:, to, bass.ds(groups[jj], SB), :] if isinstance(to, int) else
                                 nodes[:, bass.ds(to, 1), bass.ds(groups[jj], SB), :].rearrange("p l g d -> p (l g) d"))
                            nc.vector.tensor_tensor(s, s, got[:, :, 0:D], ALU.add).then_inc(bank_free, 1)

                columns(layer, 0, 0, 0)
                for k in range(LOOKAHEAD):
                    one_hot(k)
                with dve.Fori(0, ITEMS // BODY - 1) as turn:
                    body(turn, False)
                body(ITEMS // BODY - 1, True)
                dve.wait_ge(bank_free, (layer + 1) * ITEMS + BANKS)

            with dve.Fori(0, LIGHT - 1) as l:
                dve.wait_ge(cleared, l + 1)
                add_layer(l, l, False)
                nc.vector.tensor_tensor(nodes[:, TOTAL, :, :], nodes[:, TOTAL, :, :],
                                        nodes[:, bass.ds(l, 1), :, :].rearrange("p l g d -> p (l g) d"), ALU.add).then_inc(summed, 1)
                dve.wait_ge(summed, l + 1)
            add_layer(LIGHT - 1, TOTAL, False)

            def norm(n):
                def wide(v, q):
                    return v.unsqueeze(2).to_broadcast([P, PART[q + 1] - PART[q], D])
                for q in range(Q):
                    gs = slice(PART[q], PART[q + 1])
                    if n == 1:
                        dve.wait_ge(dense_out, 2 + STEPS + PART[q + 1] // DB)
                    link(nc.vector.tensor_reduce(sum_f[:, gs], nodes[:, TOTAL, gs, :], AX.X, ALU.add))
                    link(nc.vector.tensor_scalar(stage[2][:, gs], sum_f[:, gs], 1.0 / D, None, ALU.mult))
                    nc.vector.tensor_tensor(nodes[:, TOTAL, gs, :], nodes[:, TOTAL, gs, :], wide(stage[2][:, gs], q),
                                            ALU.subtract).then_inc(centred, 1)
                for q in range(Q):
                    gs = slice(PART[q], PART[q + 1])
                    dve.wait_ge(squared, n * Q + q + 1)
                    link(nc.vector.tensor_reduce(sum_f[:, gs], nodes[:, XNODES if n == 0 else 0, gs, :], AX.X, ALU.add))
                    nc.vector.tensor_scalar(rstd[:, gs], sum_f[:, gs], 1.0 / (D * (LIGHT + 1) ** 2) if n == 0 else 1.0 / D, EPS,
                                            ALU.mult, ALU.add).then_inc(var_set, 1)
                for q in range(Q):
                    gs = slice(PART[q], PART[q + 1])
                    dve.wait_ge(std_set, n * Q + q + 1)
                    link(nc.vector.reciprocal(stage[2][:, gs], rstd[:, gs]))
                    nc.vector.tensor_tensor(nodes[:, TOTAL, gs, :], nodes[:, TOTAL, gs, :], wide(stage[2][:, gs], q),
                                            ALU.mult).then_inc(normed, 1)

            norm(0)
            link(nc.vector.memset(edge_t[:, :, 1], 1.0))
            dve.wait_ge(cleared, 3)
            add_layer(LIGHT, 0, True)
            dve.wait_ge(deg_added, ITEMS)
            link(nc.vector.tensor_scalar(rdeg[:, :], degree[:, :], 1.0, None, ALU.max))
            link(nc.vector.reciprocal(rdeg[:, :], rdeg[:, :]))
            link(nc.vector.tensor_copy(stage[2][:, 0:G], rdeg[:, :]))

            def means(l, half):
                def step(n, h):
                    dve.wait_ge(cat_T, n + (l * STEPS + 1))
                    gs = bass.ds(n * DB, DB)
                    nc.vector.tensor_tensor(both[:, h, :, D:2 * D], nodes[:, half, gs, :],
                                            stage[2][:, gs].unsqueeze(2).to_broadcast([P, DB, D]), ALU.mult).then_inc(mean_ready, 1)
                steps(dve, step)

            means(0, 0)
            dve.wait_ge(cleared, 4)
            add_layer(LIGHT + 1, 1, False)
            means(1, 1)
            norm(1)


ARGS = ["x", "src", "dst", "edge_weight", "L1_gnn_W_self1", "L1_gnn_W_neigh1", "L1_gnn_b1",
        "L1_gnn_W_self2", "L1_gnn_W_neigh2", "L1_gnn_b2"]


def kernel(**inputs):
    import concourse.bacc as bacc
    from concourse.bass_utils import run_bass_kernel_spmd

    nc = bacc.Bacc("TRN2", target_bir_lowering=False, num_devices=1)
    arrays, args = {}, []
    for name in ARGS:
        a = np.ascontiguousarray(inputs[name])
        arrays[f"in_{name}"] = a
        args.append(nc.dram_tensor(f"in_{name}", a.shape, mybir.dt.from_np(a.dtype), kind="ExternalInput").ap())
    args.append(nc.dram_tensor("out", (N, D), F32, kind="ExternalOutput").ap())
    build_program(nc, *args)
    result = run_bass_kernel_spmd(nc, [arrays], core_ids=[0])
    return result.results[0]["out"]
```

```python
from contextlib import ExitStack

import numpy as np

import concourse.bass as bass
from concourse import mybir

F32 = mybir.dt.float32
I32 = mybir.dt.int32
U16 = mybir.dt.uint16
BF16 = mybir.dt.bfloat16
ALU = mybir.AluOpType
ACT = mybir.ActivationFunctionType
AX = mybir.AxisListType

P = 128
N, D, E = 15625, 64, 250000
LIGHT, SAGE = 3, 2
LAYERS = LIGHT + SAGE
EPS = 1e-5

SB = 2
BN = SB * P
NB = -(-N // BN)
G = NB * SB
WHOLE = N // P
NPAD = G * P
ROWS = -(-E // P)
FULL = E // P
LAST = E - FULL * P
CH = 16
BODY = 2 * CH
ITEMS = -(-(ROWS + NB - 1) // BODY) * BODY
RCH = -(-ROWS // CH)
SETS = -(-ITEMS // P)
SLOTS = SETS * P
RING = P
SEMS = 2 * CH
HOTS = 8
LOOKAHEAD = 4
BANKS = 4
COUNT_P, COUNT_F = 125, E // 125
DVE_COUNTS = 40
TABLES_AT = 5
BUFS = 4
NOWHERE = 1 << 20
DB = 4
STEPS = G // DB
Q = 4
LEAD = 6
PART = [0, 48, 88, 112, G]
assert ITEMS // BODY == 2 * STEPS + 1 and RCH == 4 * (STEPS - 2) + LEAD + 1
assert RCH % 2 == 1 and STEPS % 2 == 1 and ROWS % SEMS == 2 and RING >= NB + 4 * CH
XNODES = 3
TOTAL = 2


def build_program(nc, x, src, dst, edge_weight, w_self1, w_neigh1, b1, w_self2, w_neigh2, b2, out):
    table = [x] + [nc.dram_tensor(f"table{l}", (NPAD, D), F32, kind="Internal").ap() for l in range(1, LAYERS)]
    table_p = [None] + [t.rearrange("(p g) d -> p g d", p=P) for t in table[1:]]
    edges = nc.dram_tensor("edges", (SLOTS, 2 * P), I32, kind="Internal").ap()
    edges_a = edges.rearrange("r (a e) -> r a e", a=2)
    by_block = nc.dram_tensor("by_block", (3 * E, 1), I32, kind="Internal").ap()
    by_block_a = by_block.rearrange("(a e) o -> a (e o)", a=3)

    ctx = ExitStack()
    with ctx:
        def sb(name, shape, dt=F32):
            return ctx.enter_context(nc.sbuf_tensor(name, shape, dt))

        def ps(name, shape, dt=F32):
            return ctx.enter_context(nc.psum_tensor(name, shape, dt))

        def sem(name):
            return ctx.enter_context(nc.semaphore(name))

        nodes = sb("nodes", [P, 4, G, D])
        degree = sb("degree", [P, G])
        src_t = sb("src_t", [P, SLOTS], U16)
        edge_t = sb("edge_t", [P, SLOTS, 2])
        item_regs = sb("item_regs", [3, SLOTS], U16)
        index = sb("index", [P, 2, CH], I32)
        edge_c = sb("edge_c", [P, 2, CH, 2])
        msg = sb("msg", [P, RING, D + 1])
        hot = sb("hot", [P, HOTS, BN])
        ident = sb("ident", [P, P])
        ones = sb("ones", [P, P])
        zero = sb("zero", [P, 1])
        weights = sb("weights", [P, 2, 2, 2 * D])
        bias = sb("bias", [1, 2, DB, D])
        count = sb("count", [P, NB + 1])
        edge_at = sb("edge_at", [P, NB + 1])
        edge_i = sb("edge_i", [P, NB + 1], I32)
        row_i = sb("row_i", [P, NB + 1], I32)
        row_at = sb("row_at", [P, NB + 1])
        last_f = sb("last_f", [P, NB])
        last_i = sb("last_i", [P, NB], I32)
        filled = sb("filled", [P, NB])
        rows_of = sb("rows_of", [P, NB])
        item_at = sb("item_at", [P, NB + 1])
        item_at_i = sb("item_at_i", [1, NB + 1], I32)
        begun_by = sb("begun_by", [1, RING // CH])
        begun_by_i = sb("begun_by_i", [1, RING // CH], I32)
        lag = sb("lag", [P, NB])
        slip = sb("slip", [P, NB - 1])
        zeros_b = sb("zeros_b", [P, NB])
        below_act = sb("below_act", [P, NB])
        block_i = sb("block_i", [P, NB], I32)
        starts = sb("starts", [P, NB])
        item_i = sb("item_i", [P, SETS], I32)
        item_f = sb("item_f", [P, SETS])
        block_f = sb("block_f", [P, SETS])
        first_dst = sb("first_dst", [P, SETS])
        shift = sb("shift", [P, SETS])
        row_f = sb("row_f", [P, SETS])
        row_of = sb("row_of", [P, SETS], I32)
        held_i = sb("held_i", [P, SETS], I32)
        regs_f = sb("regs_f", [P, 3, SETS])
        pick = sb("pick", [P, BUFS], I32)
        rstd = sb("rstd", [P, G])
        sum_f = sb("sum_f", [P, G])
        rdeg = rstd
        mean = sb("mean", [P, 2, DB * D])
        own = sb("own", [P, DB * D])
        turned = sb("turned", [P, 2, DB * P])
        rows = hot[:, 4:8, :].bitcast(I32).rearrange("p h (a e) -> p h a e", a=2)
        rowf = turned[:, 0, :].rearrange("p (h e) -> p h e", h=BUFS)
        iota_i = turned[:, 1, 0:BN].bitcast(I32)
        regs_i = turned[0:3 * SETS, 1, BN:BN + P // 2].bitcast(U16)
        room = nodes[:, 1, :, :].rearrange("p g d -> p (g d)")
        dst_i = room[0:COUNT_P, 0:COUNT_F].bitcast(I32)
        dst_f = room[0:COUNT_P, COUNT_F:2 * COUNT_F]
        at = 2 * COUNT_F
        below = room[0:COUNT_P, at:at + COUNT_F // 2].bitcast(BF16)
        signs = room[0:COUNT_P, at + COUNT_F // 2:at + COUNT_F].bitcast(BF16)
        at += COUNT_F
        tail = room[0:SLOTS - FULL, at:at + 2 * P].bitcast(I32).rearrange("p (a e) -> p a e", a=2)
        at += 2 * P
        src_x = room[:, at:at + SLOTS // 2].bitcast(U16)
        begun, slips = (room[:, n * SETS * (NB - 1):(n + 1) * SETS * (NB - 1)].rearrange("p (k b) -> p k b", k=SETS)
                        for n in range(2))
        src_rows, low, high = (nodes[:, 0, :, :].rearrange("p g d -> p (g d)")[:, n * SLOTS:(n + 1) * SLOTS].bitcast(I32)
                               for n in range(3))
        src_f = nodes[:, XNODES, :, :].rearrange("p g d -> p (g d)")[:, 0:SLOTS]

        next_dst = sb("next_dst", [COUNT_P, 1], I32)
        falls = sb("falls", [P, 2])
        unsorted_i = sb("unsorted_i", [1, 1], I32)
        before = hot[:, 0, 0:P]
        reached = hot[:, 1, 0:NB + 1]
        inside = hot[:, 2, 0:NB]
        filled_to = hot[:, 3, 0:NB]
        rank = hot[:, 4, 0:NB]
        place = hot[:, 5, 0:1]
        dst_e = hot[:, 5, 1:2]
        lists_at = hot[:, 5, 4:7]
        edge_e = hot[:, 6, 0:3].bitcast(I32)
        place_i = hot[:, 7, 0:3].bitcast(I32)

        iota_p = ps("iota_p", [P, BN])
        sums = [ps(f"sums{i}", [P, 512]) for i in range(BANKS)]
        stage = [ps(f"stage{i}", [P, 512]) for i in range(3)]

        x_in, dst_in, par_in, tail_in, edges_out, src_in = (
            sem(n) for n in ("x_in", "dst_in", "par_in", "tail_in", "edges_out", "src_in"))
        pads_set, tail_set, iota_set, item_set, ident_set = (
            sem(n) for n in ("pads_set", "tail_set", "iota_set", "item_set", "ident_set"))
        dve_chain = sem("dve_chain")
        src_split, src_done, src_T, src_tab = (sem(n) for n in ("src_split", "src_done", "src_T", "src_tab"))
        falls_set, falls_sum, order_known, next_in = (sem(n) for n in ("falls_set", "falls_sum", "order_known", "next_in"))
        before_set, sort_chain, sort_count, edge_in, inside_set, ranked, placed, row_sorted, resorted = (
            sem(n) for n in ("before_set", "sort_chain", "sort_count", "edge_in", "inside_set", "ranked", "placed",
                             "row_sorted", "resorted"))
        scattered = [sem(f"{a}_scattered") for a in ("src", "dst", "weight")]
        starts_set, signed = sem("starts_set"), sem("signed")
        counted, edge_sum, rows_set, regs_ready, regs_T, regs_copied, regs_in = (
            sem(n) for n in ("counted", "edge_sum", "rows_set", "regs_ready", "regs_T", "regs_copied", "regs_in"))
        picked, row_done, row_T = sem("picked"), sem("row_done"), sem("row_T")
        rows_in = [sem(f"rows_in{h}") for h in range(BUFS)]
        tab_done = sem("tab_done")
        total_set = sem("total_set")
        cleared = sem("cleared")
        layer_in = sem("layer_in")
        idx_ready = sem("idx_ready")
        landed = [sem(f"landed{j}") for j in range(SEMS)]
        rows_landed = sem("rows_landed")
        cols_in = sem("cols_in")
        hot_ready = sem("hot_ready")
        items_done = sem("items_done")
        bank_free = sem("bank_free")
        deg_added, summed = sem("deg_added"), sem("summed")
        paced = sem("paced")
        centred, squared, var_set, std_set, normed = (sem(n) for n in ("centred", "squared", "var_set", "std_set", "normed"))
        own_ready, self_turned, self_copied, self_done, self_out = (
            sem(n) for n in ("own_ready", "self_turned", "self_copied", "self_done", "self_out"))
        early_items = sem("early_items")
        degrees_known, weights_clear = sem("degrees_known"), sem("weights_clear")
        mean_ready, mean_turned, mean_copied = sem("mean_ready"), sem("mean_turned"), sem("mean_copied")
        dense_done, dense_out, hidden_ready = sem("dense_done"), sem("dense_out"), sem("hidden_ready")
        out_done = sem("out_done")
        block = ctx.enter_context(nc.Block())

        def steps(eng, body):
            with eng.Fori(0, STEPS // 2) as two:
                body(two * 2, 0)
                body(two * 2 + 1, 1)
            body(STEPS - 1, 0)

        def if_unsorted(eng):
            eng.wait_ge(order_known, 1)
            return eng.If(eng.value_load(unsorted_i[0:1, 0:1], min_val=0, max_val=E) > 0)

        def each_row(eng, body):
            with eng.Fori(0, FULL) as r:
                body(r, P)
            body(FULL, LAST)

        @block.sync
        def _(sp):
            sp.dma_start(dst_i, dst.rearrange("(p f) -> p f", p=COUNT_P)).then_inc(dst_in, 16)
            sp.dma_start(next_dst[0:COUNT_P - 1, :], dst.rearrange("(p f) -> p f", p=COUNT_P)[1:COUNT_P, 0:1],
                         allow_slow_non_contiguous=True).then_inc(next_in, 16)

            def load_src_rows(list_, signal):
                into = src_rows.rearrange("p (k e) -> p k e", k=SETS)
                r0 = (SETS - 1) * P
                sp.dma_start(into[:, 0:SETS - 1, :], list_[0:r0 * P].rearrange("(k p e) -> p k e", p=P, e=P)).then_inc(signal, 16)
                sp.dma_start(into[0:FULL - r0, SETS - 1, :], list_[r0 * P:FULL * P].rearrange("(r e) -> r e", e=P)).then_inc(signal, 16)
                sp.dma_start(into[FULL - r0:FULL - r0 + 1, SETS - 1, 0:LAST],
                             list_[FULL * P:E].rearrange("(r e) -> r e", r=1)).then_inc(signal, 16)

            sp.wait_ge(pads_set, 1)
            load_src_rows(src, src_in)
            lists = (dst, edge_weight.bitcast(I32))
            for a, arr in enumerate(lists):
                sp.dma_start(edges_a[0:FULL, a, :], arr[0:FULL * P].rearrange("(r e) -> r e", e=P)).then_inc(edges_out, 16)
            sp.wait_ge(tail_set, 2)
            for a, arr in enumerate(lists):
                sp.dma_start(tail[0:1, a, 0:LAST], arr[FULL * P:E].rearrange("(r e) -> r e", r=1)).then_inc(tail_in, 16)
            sp.wait_ge(tail_in, 32)
            sp.dma_start(edges_a[FULL:SLOTS, :, :], tail).then_inc(edges_out, 16)
            with if_unsorted(sp):
                def load(r, n):
                    for a, arr in enumerate((src, dst, edge_weight.bitcast(I32))):
                        sp.wait_ge(row_sorted, r + 1)
                        at = bass.ds(r * P, n)
                        sp.dma_start(edge_e[0:n, a:a + 1], arr[at].rearrange("(p o) -> p o", o=1)).then_inc(edge_in, 16)
                each_row(sp, load)
                sp.wait_ge(row_sorted, ROWS + 1)
                sp.wait_ge(edges_out, 48)
                sp.wait_ge(src_in, 48)
                load_src_rows(by_block_a[0], resorted)
                for a in range(2):
                    sp.dma_start(edges_a[0:FULL, a, :], by_block_a[1 + a, 0:FULL * P].rearrange("(r e) -> r e", e=P)).then_inc(resorted, 16)
                    sp.dma_start(edges_a[FULL:ROWS, a, 0:LAST], by_block_a[1 + a, FULL * P:E].rearrange("(r e) -> r e", r=1)).then_inc(resorted, 16)
                sp.wait_ge(resorted, 16 * 7)
            sp.wait_ge(src_T, SETS // 4)
            sp.wait_ge(pads_set, 2)
            sp.dma_start(nodes[:, XNODES, 0:WHOLE, :], x[0:WHOLE * P, :].rearrange("(g p) d -> p g d", p=P)).then_inc(x_in, 16)
            sp.dma_start(nodes[0:N - WHOLE * P, XNODES, WHOLE, :], x[WHOLE * P:N, :]).then_inc(x_in, 16)
            for l, (ws, wn, b) in enumerate(((w_self1, w_neigh1, b1), (w_self2, w_neigh2, b2))):
                sp.wait_ge(weights_clear, 1)
                for at in (0, D):
                    sp.dma_start(weights[at:at + D, l, 0, at:at + D], ws).then_inc(par_in, 16)
                    sp.dma_start(weights[at:at + D, l, 1, at:at + D], wn).then_inc(par_in, 16)
                for g in range(DB):
                    sp.dma_start(bias[:, l, g, :], b.rearrange("(r d) -> r d", r=1)).then_inc(par_in, 16)

            def relay(layer):
                def row(j, use):
                    sp.wait_ge(landed[j], use * 16)
                    sp.sem_inc(rows_landed, 1)
                uses = [len(range(j, ROWS, SEMS)) for j in range(SEMS)]
                with sp.Fori(0, ROWS // SEMS) as turn:
                    for j in range(SEMS):
                        row(j, turn + (layer * uses[j] + 1))
                for j in range(ROWS % SEMS):
                    row(j, (layer + 1) * uses[j])

            for l in range(LAYERS):
                relay(l)
                for q in range(Q):
                    if l == LIGHT - 1:
                        sp.wait_ge(normed, q + 1)
                        sp.dma_start(table_p[LIGHT][:, PART[q]:PART[q + 1], :],
                                     nodes[:, TOTAL, PART[q]:PART[q + 1], :]).then_inc(layer_in, 16)
                    if l == LIGHT:
                        sp.wait_ge(hidden_ready, PART[q + 1] // DB)
                        sp.dma_start(table_p[LIGHT + 1][:, PART[q]:PART[q + 1], :],
                                     nodes[:, XNODES, PART[q]:PART[q + 1], :]).then_inc(layer_in, 16)
                    if l == LIGHT + 1:
                        sp.wait_ge(normed, Q + q + 1)
                        g0, g1 = PART[q], min(PART[q + 1], WHOLE)
                        sp.dma_start(out[g0 * P:g1 * P, :].rearrange("(g p) d -> p g d", p=P),
                                     nodes[:, TOTAL, g0:g1, :]).then_inc(out_done, 16)
            sp.dma_start(out[WHOLE * P:N, :], nodes[0:N - WHOLE * P, TOTAL, WHOLE, :]).then_inc(out_done, 16)
            sp.wait_ge(out_done, 16 * (Q + 1))
            sp.wait_ge(layer_in, 16 * Q * (LAYERS - 1))

        @block.gpsimd
        def _(pool):
            pool.memset(src_rows[:, (SETS - 1) * P:SLOTS], 0).then_inc(pads_set, 1)
            for a, fill in enumerate((NOWHERE, 0)):
                pool.memset(tail[:, a, :], fill).then_inc(tail_set, 1)
            pool.memset(nodes[:, XNODES, WHOLE:G, :], 0.0).then_inc(pads_set, 1)
            pool.iota(iota_i, [[1, BN]], base=0, channel_multiplier=0).then_inc(iota_set, 1)
            pool.memset(ident[:, :], 0.0).then_inc(ident_set, 1)
            pool.wait_ge(ident_set, 1)
            pool.affine_select(out=ident[:, :], in_=ident[:, :], compare_op=ALU.not_equal, fill=1.0, base=0,
                               pattern=[[-1, P]], channel_multiplier=1).then_inc(ident_set, 1)
            pool.iota(block_i[:, :], [[BN, NB]], base=0, channel_multiplier=0).then_inc(item_set, 1)
            pool.iota(item_i[:, :], [[P, SETS]], base=0, channel_multiplier=1).then_inc(item_set, 1)

            with if_unsorted(pool):
                pool.memset(before, 0.0).then_inc(before_set, 1)
                pool.wait_ge(before_set, 1)
                pool.affine_select(out=before, in_=before, compare_op=ALU.is_ge, fill=1.0, base=0,
                                   pattern=[[-1, P]], channel_multiplier=1).then_inc(before_set, 1)
                pool.sem_inc(row_sorted, 1)

                def scatter(r, n):
                    pool.wait_ge(placed, r + 1)
                    pool.sem_inc(paced, 1)
                    for a in range(3):
                        pool.indirect_dma_start(by_block, bass.IndirectOffsetOnAxis(place_i[0:n, a:a + 1], axis=0),
                                                edge_e[0:n, a:a + 1], None).then_inc(scattered[a], 16)
                    for a in range(3):
                        pool.wait_ge(scattered[a], r * 16 + 16)
                    pool.sem_inc(row_sorted, 1)
                each_row(pool, scatter)
                pool.wait_ge(resorted, 16 * 7)

            def gather_chunk(layer, c, q, first=False, before=None):
                pool.wait_ge(idx_ready, c + (layer * RCH + 1))
                if before is not None:
                    pool.wait_ge(items_done, before + HOTS)
                    pool.sem_inc(paced, 1)
                elif not first:
                    pool.wait_ge(items_done, c * CH + (layer * ITEMS + CH - RING + NB + HOTS))
                    pool.sem_inc(paced, 1)
                for j in range(CH if not isinstance(c, int) else min(CH, ROWS - c * CH)):
                    pool.indirect_dma_start(msg[:, q * CH + j, 0:D], None, table[layer],
                                            bass.IndirectOffsetOnAxis(index[:, q % 2, j:j + 1], axis=0)
                                            ).then_inc(landed[q % 2 * CH + j], 16)

            per = RING // CH
            for l in range(LAYERS):
                if l:
                    pool.wait_ge(layer_in, l * Q * 16)
                for q in range(TABLES_AT if l == 0 else per):
                    gather_chunk(l, q, q, first=True)
                if l == 0:
                    pool.wait_ge(edges_out, 48)
                    pool.wait_ge(rows_set, 1)
                    with pool.Fori(0, SETS // BUFS) as some:
                        for h in range(BUFS):
                            pool.wait_ge(tab_done, some * BUFS + (h + 1))
                            pool.tensor_copy(pick[:, h:h + 1], row_of[:, bass.ds(some * BUFS + h, 1)]).then_inc(picked, 1)
                            pool.wait_ge(picked, some * BUFS + (h + 1))
                            pool.sem_inc(paced, 1)
                            pool.indirect_dma_start(rows[:, h, :, :].rearrange("p a e -> p (a e)"), None, edges,
                                                    bass.IndirectOffsetOnAxis(pick[:, h:h + 1], axis=0)).then_inc(rows_in[h], 16)
                    for q in range(TABLES_AT, per):
                        gather_chunk(l, q, q, first=True)
                    pool.wait_ge(early_items, 1)
                    for q in range(per):
                        items = pool.value_load(begun_by_i[0:1, q:q + 1], min_val=1, max_val=ITEMS)
                        gather_chunk(l, per + q, q, before=items)
                with pool.Fori(1 if l else 2, RCH // per) as turn:
                    for q in range(per):
                        gather_chunk(l, turn * per + q, q)
                for c in range(RCH // per * per, RCH):
                    gather_chunk(l, c, c % per)
                if l >= LIGHT:
                    half = l - LIGHT
                    if half == 0:
                        pool.wait_ge(degrees_known, 1)
                    pool.wait_ge(bank_free, (l + 1) * ITEMS + BANKS)

                    def means(n, h):
                        pool.wait_ge(mean_turned, n + (half * STEPS + 1))
                        gs = bass.ds(n * DB, DB)
                        pool.tensor_tensor(mean[:, h, :].rearrange("p (g d) -> p g d", g=DB), nodes[:, half, gs, :],
                                           rdeg[:, gs].unsqueeze(2).to_broadcast([P, DB, D]), ALU.mult).then_inc(mean_ready, 1)
                    steps(pool, means)

        @block.tensor
        def _(pe):
            pe.wait_ge(falls_set, 1)
            nc.tensor.matmul(stage[2][:, 0:2], ones[:, :], falls[:, :], start=True, stop=True).then_inc(falls_sum, 1)
            with if_unsorted(pe):
                pe.wait_ge(sort_count, 1)
                nc.tensor.matmul(stage[0][:, 0:NB + 1], ones[:, :], count[:, :], start=True, stop=True).then_inc(ranked, 1)
                pe.wait_ge(before_set, 2)

                def rank_edges(r, n):
                    pe.wait_ge(inside_set, r + 1)
                    nc.tensor.matmul(stage[0][0:n, 0:NB], before[0:n, 0:n], inside[0:n, :], start=True, stop=True)
                    nc.tensor.matmul(stage[1][:, 0:NB], ones[0:n, :], inside[0:n, :], start=True, stop=True).then_inc(ranked, 1)
                each_row(pe, rank_edges)
            pe.wait_ge(ident_set, 2)
            for four in range(2 * SETS // 4):
                if four % (SETS // 4) == 0:
                    pe.wait_ge(src_done, 1 + four // (SETS // 4))
                rows_f = src_f if four < SETS // 4 else high.bitcast(F32)
                if four >= 2:
                    pe.wait_ge(src_tab, four - 1)
                for k in range(4):
                    c = (four % (SETS // 4) * 4 + k) * P
                    tr = nc.tensor.transpose(stage[four % 2][:, k * P:(k + 1) * P], rows_f[:, c:c + P], ident[:, :])
                tr.then_inc(src_T, 1)
            pe.wait_ge(counted, 2)
            nc.tensor.matmul(stage[2][:, 0:NB + 1], ones[:, :], count[:, :], start=True, stop=True).then_inc(edge_sum, 1)
            pe.wait_ge(regs_ready, 1)
            nc.tensor.transpose(stage[2][0:3 * SETS, 0:P], regs_f[:, :, :].rearrange("p a k -> p (a k)"), ident[:, :]).then_inc(regs_T, 1)
            with pe.Fori(0, SETS // BUFS) as some:
                for h in range(BUFS):
                    pe.wait_ge(row_done, some * BUFS + (h + 1))
                    pe.wait_ge(tab_done, some * BUFS + (h + 1))
                    nc.tensor.transpose(sums[h][:, 0:P], rowf[:, h, :], ident[:, :])
                    nc.tensor.transpose(sums[h][:, P:2 * P], rows[:, h, 1, :].bitcast(F32), ident[:, :]).then_inc(row_T, 1)
            pe.wait_ge(regs_in, 48)
            flat = msg[:, :, :].rearrange("p r d -> p (r d)")

            def slots(at):
                return nc.values_load_multi_w_load_instructions(
                    item_regs[1:2, bass.ds(at, CH)], engines=[mybir.EngineType.PE], min_val=0, max_val=(RING - 1) * (D + 1),
                    skip_runtime_bounds_check_because="a slot is a row's low bits")[1]

            def rows_needed(at):
                return nc.values_load_multi_w_load_instructions(
                    item_regs[2:3, bass.ds(at + 3, CH // 4, 4)], engines=[mybir.EngineType.PE], min_val=1, max_val=ROWS)[1]

            def sum_items(layer, width, first, last):
                with pe.Fori(first, last) as turn:
                    i = turn * BODY + layer * ITEMS
                    for h in range(2):
                        at = slots(turn * BODY + h * CH)
                        need = rows_needed(turn * BODY + h * CH)
                        for jj in range(CH):
                            j = h * CH + jj
                            if j % 4 == 0:
                                pe.wait_ge(rows_landed, need[jj // 4] + layer * ROWS)
                            if j % 2 == 0:
                                pe.wait_ge(bank_free, i + (j + 2))
                                pe.wait_ge(hot_ready, i + (j + 2))
                            for g in range(SB):
                                mm = nc.tensor.matmul(sums[j % BANKS][:, g * width:(g + 1) * width],
                                                      hot[:, j % HOTS, g * P:(g + 1) * P],
                                                      flat[:, bass.ds(at[jj], width)], start=True, stop=True)
                            mm.then_inc(items_done, 1)

            def turn_self(l, n):
                pe.wait_ge(own_ready, n + (l * STEPS + 1))
                for two in range(DB // 2):
                    tr = nc.tensor.transpose(stage[0][:, two * P:(two + 1) * P], own[:, two * P:(two + 1) * P], ident[:, :])
                tr.then_inc(self_turned, 1)

            def product_self(l, n):
                pe.wait_ge(self_copied, n + (l * STEPS + 1))
                pe.wait_ge(self_out, n + (l * STEPS + 1))
                nc.tensor.matmul(stage[2][:, 0:DB * D], ones[0:1, :], bias[:, l, :, :].rearrange("p g d -> p (g d)"),
                                 start=True, stop=False)
                if l == 1:
                    nc.tensor.matmul(stage[2][:, 0:DB * D], ident[:, :],
                                     nodes[:, TOTAL, bass.ds(n * DB, DB), :].rearrange("p g d -> p (g d)"),
                                     start=False, stop=False)
                for two in range(DB // 2):
                    mm = nc.tensor.matmul(stage[2][:, two * P:(two + 1) * P], turned[:, 0, two * P:(two + 1) * P],
                                          weights[:, l, 0, :], start=False, stop=two == DB // 2 - 1)
                mm.then_inc(self_done, 1)

            def sage_layer(l, width):
                layer = LIGHT + l
                turn_self(l, 0)
                with pe.Fori(0, STEPS - 1) as n:
                    sum_items(layer, width, n * 2, n * 2 + 2)
                    product_self(l, n)
                    turn_self(l, n + 1)
                sum_items(layer, width, 2 * STEPS - 2, 2 * STEPS)
                product_self(l, STEPS - 1)
                sum_items(layer, width, 2 * STEPS, ITEMS // BODY)

            def dense(l):
                def turn_over(n, h):
                    t = n + l * STEPS
                    pe.wait_ge(mean_ready, t + 1)
                    pe.wait_ge(mean_copied, t + 1)
                    for two in range(DB // 2):
                        tr = nc.tensor.transpose(stage[h][:, two * P:(two + 1) * P], mean[:, h, two * P:(two + 1) * P], ident[:, :])
                    tr.then_inc(mean_turned, 1)

                def product(n, h):
                    t = n + l * STEPS
                    pe.wait_ge(mean_copied, t + 3)
                    pe.wait_ge(dense_out, t + 1)
                    for two in range(DB // 2):
                        mm = nc.tensor.matmul(sums[h][:, two * P:(two + 1) * P], turned[:, h, two * P:(two + 1) * P],
                                              weights[:, l, 1, :], start=True, stop=True)
                    mm.then_inc(dense_done, 1)

                turn_over(0, 0)
                with pe.Fori(0, STEPS // 2) as two:
                    turn_over(two * 2 + 1, 1)
                    product(two * 2, 0)
                    turn_over(two * 2 + 2, 0)
                    product(two * 2 + 1, 1)
                product(STEPS - 1, 0)

            with pe.Fori(0, LIGHT) as l:
                sum_items(l, D, 0, ITEMS // BODY)
            pe.wait_ge(par_in, 16 * 2 * (4 + DB))
            pe.wait_ge(normed, Q)
            sage_layer(0, D + 1)
            dense(0)
            pe.wait_ge(hidden_ready, STEPS)
            sage_layer(1, D)
            dense(1)

        @block.scalar
        def _(act):
            def node_row(n):
                return nodes[:, n, :, :].rearrange("p g d -> p (g d)")

            def clear(n):
                nc.scalar.activation(node_row(n), zero[:, 0:1].to_broadcast([P, G * D]), ACT.Copy).then_inc(cleared, 1)

            def src_columns(n):
                to = (src_x if n < SETS // 4 else src_t[:, :])
                c = n % (SETS // 4) * 512
                act.wait_ge(src_T, n + 1)
                nc.scalar.activation(to[:, c:c + 512], stage[n % 2][:, :], ACT.Copy).then_inc(src_tab, 1)

            def index_chunk(layer, c, h):
                act.wait_ge(rows_landed, c * CH + (layer * ROWS - CH + 1))
                nc.scalar.activation(index[:, h, :], (src_t[:, :] if layer else src_x)[:, bass.ds(c * CH, CH)],
                                     ACT.Copy).then_inc(idx_ready, 1)

            def index_chunks(layer, c0, c1):
                with act.Fori(c0 // 2, c1 // 2) as two:
                    index_chunk(layer, two * 2 + 1, 1)
                    index_chunk(layer, two * 2 + 2, 0)

            for n in range(SETS // 4):
                src_columns(n)
            act.wait_ge(src_tab, SETS // 4)
            nc.scalar.activation(index[:, 0, :], src_x[:, 0:CH], ACT.Copy).then_inc(idx_ready, 1)
            for n in range(SETS // 4, 2 * SETS // 4):
                src_columns(n)
            act.wait_ge(starts_set, 2)
            early = TABLES_AT + 1
            for b in range(DVE_COUNTS, NB):
                c = (b - DVE_COUNTS) // 4 + 1
                if (b - DVE_COUNTS) % 4 == 0 and c < early:
                    index_chunk(0, c, c % 2)
                if b > DVE_COUNTS:
                    act.wait_ge(signed, b - DVE_COUNTS)
                nc.scalar.activation(signs, dst_f, ACT.Sign, bias=starts[0:COUNT_P, b:b + 1], scale=-1.0,
                                     accum_out=below_act[0:COUNT_P, b:b + 1]).then_inc(signed, 1)
            act.wait_ge(x_in, 32)
            nc.scalar.activation(node_row(TOTAL), node_row(XNODES), ACT.Copy, scale=float(LIGHT + 2)).then_inc(total_set, 1)
            clear(0)
            for c in range(min(len(range(DVE_COUNTS, NB, 4)) + 1, early), early):
                index_chunk(0, c, c % 2)
            act.wait_ge(regs_T, 1)
            nc.scalar.activation(regs_i, stage[2][0:3 * SETS, 0:P], ACT.Copy).then_inc(regs_copied, 1)
            act.wait_ge(regs_copied, 1)
            for n in range(3):
                act.dma_start(item_regs[n:n + 1, :].rearrange("r (k p) -> r k p", k=SETS),
                              regs_i[n * SETS:(n + 1) * SETS, :]).then_inc(regs_in, 16)
            with act.Fori(0, SETS // BUFS) as some:
                for h in range(BUFS):
                    act.wait_ge(row_T, some * BUFS + (h + 1))
                    nc.scalar.activation(edge_t[:, bass.ds((some * BUFS + h) * P, P), :].rearrange("p c a -> p a c"),
                                         sums[h][:, 0:2 * P].rearrange("p (a c) -> p a c", a=2), ACT.Copy).then_inc(tab_done, 1)
            for c in range(early, RING // CH + 1):
                index_chunk(0, c, c % 2)

            def norm(n, squares, scale):
                for q in range(Q):
                    gs = slice(PART[q], PART[q + 1])
                    act.wait_ge(centred, n * Q + q + 1)
                    nc.scalar.activation(nodes[:, squares, gs, :], nodes[:, TOTAL, gs, :], ACT.Square).then_inc(squared, 1)
                for q in range(Q):
                    gs = slice(PART[q], PART[q + 1])
                    act.wait_ge(var_set, n * Q + q + 1)
                    nc.scalar.activation(rstd[:, gs], rstd[:, gs], ACT.Sqrt, scale=scale).then_inc(std_set, 1)

            def take_own(l, n):
                if not isinstance(n, int) or n:
                    act.wait_ge(self_turned, n + l * STEPS)
                nc.scalar.activation(own[:, :].rearrange("p (g d) -> p g d", g=DB),
                                     nodes[:, XNODES if l else TOTAL, bass.ds(n * DB, DB), :], ACT.Copy).then_inc(own_ready, 1)

            def copy_self(l, n):
                act.wait_ge(self_turned, n + (l * STEPS + 1))
                nc.scalar.activation(turned[:, 0, 0:DB // 2 * P], stage[0][:, 0:DB // 2 * P], ACT.Copy).then_inc(self_copied, 1)

            def keep_self(l, n):
                act.wait_ge(self_done, n + (l * STEPS + 1))
                nc.scalar.activation(nodes[:, XNODES, bass.ds(n * DB, DB), :],
                                     stage[2][:, 0:DB * D].rearrange("p (g d) -> p g d", g=DB), ACT.Copy).then_inc(self_out, 1)

            def sage_chunks(l):
                layer = LIGHT + l
                take_own(l, 0)
                copy_self(l, 0)
                take_own(l, 1)
                index_chunks(layer, 0, LEAD)
                with act.Fori(0, STEPS - 2) as n:
                    keep_self(l, n)
                    copy_self(l, n + 1)
                    take_own(l, n + 2)
                    for c in (LEAD + 1, LEAD + 3):
                        index_chunk(layer, n * 4 + c, 1)
                        index_chunk(layer, n * 4 + (c + 1), 0)
                for n in (STEPS - 2, STEPS - 1):
                    keep_self(l, n)
                    if n + 1 < STEPS:
                        copy_self(l, n + 1)

            def dense(l):
                def columns(n, h):
                    act.wait_ge(mean_turned, n + (l * STEPS + 3))
                    nc.scalar.activation(turned[:, h, 0:DB // 2 * P], stage[h][:, 0:DB // 2 * P], ACT.Copy).then_inc(mean_copied, 1)

                def result(n, h):
                    if l == 0:
                        act.wait_ge(dense_out, n + 3)
                        gs = bass.ds(n * DB, DB)
                        nc.scalar.activation(nodes[:, XNODES, gs, :], nodes[:, XNODES, gs, :], ACT.Relu).then_inc(hidden_ready, 1)

                columns(0, 0)
                with act.Fori(0, STEPS // 2) as two:
                    columns(two * 2 + 1, 1)
                    result(two * 2, 0)
                    columns(two * 2 + 2, 0)
                    result(two * 2 + 1, 1)
                result(STEPS - 1, 0)

            for l in range(LAYERS):
                if l:
                    act.wait_ge(rows_landed, l * ROWS)
                    nc.scalar.activation(index[:, 0, :], src_t[:, 0:CH], ACT.Copy).then_inc(idx_ready, 1)
                if l == LIGHT + 1:
                    act.wait_ge(layer_in, (LAYERS - 1) * Q * 16)
                if l == LIGHT:
                    act.wait_ge(normed, Q)
                if l < LIGHT:
                    index_chunks(l, 0 if l else RING // CH, RCH)
                else:
                    sage_chunks(l - LIGHT)
                if l == 0:
                    act.wait_ge(tab_done, BUFS + SETS)
                    act.wait_ge(idx_ready, RCH)
                    clear(1)
                if l in (1, 2):
                    act.wait_ge(summed, l)
                    clear(l - 1)
                if l < LIGHT - 1:
                    for q in range(Q):
                        if q < Q - 1:
                            upto = act.value_load(item_at_i[0:1, PART[q + 1] // SB:PART[q + 1] // SB + 1], min_val=0, max_val=ITEMS)
                            act.wait_ge(bank_free, upto + (l * ITEMS + BANKS))
                        else:
                            act.wait_ge(bank_free, (l + 1) * ITEMS + BANKS)
                        act.dma_start(table_p[l + 1][:, PART[q]:PART[q + 1], :],
                                      nodes[:, l, PART[q]:PART[q + 1], :]).then_inc(layer_in, 16)
                if l == LIGHT - 1:
                    norm(0, XNODES, float((LIGHT + 1) ** 2))
                if l == LIGHT:
                    dense(0)
                if l == LIGHT + 1:
                    dense(1)
                    norm(1, 0, 1.0)

        @block.vector
        def _(dve):
            chained = [0]

            def link(ins):
                chained[0] += 1
                ins.then_inc(dve_chain, 1)
                dve.wait_ge(dve_chain, chained[0])

            nc.vector.memset(ones[:, :], 1.0)
            nc.vector.memset(weights[:, :, :, :], 0.0).then_inc(weights_clear, 1)
            nc.vector.memset(zero[:, :], 0.0)
            nc.vector.memset(degree[:, :], 0.0)
            nc.vector.memset(zeros_b[:, :], 0.0)
            nc.vector.memset(item_at[:, 0:1], 0.0)
            nc.vector.memset(msg[:, :, D:D + 1], 1.0)
            link(nc.vector.memset(count[:, :], 0.0))
            link(nc.vector.memset(count[0:COUNT_P, NB:NB + 1], float(COUNT_F)))
            dve.sem_inc(items_done, HOTS)
            dve.sem_inc(bank_free, BANKS)
            dve.sem_inc(tab_done, BUFS)
            dve.sem_inc(self_out, 1)
            for ready in (mean_turned, mean_copied, dense_out):
                dve.sem_inc(ready, 2)
            link(nc.vector.memset(falls[:, :], 0.0))
            dve.wait_ge(dst_in, 16)
            link(nc.vector.tensor_copy(dst_f, dst_i))
            dve.sem_inc(starts_set, 1)
            link(nc.vector.tensor_tensor(below[:, 0:COUNT_F - 1], dst_f[:, 0:COUNT_F - 1], dst_f[:, 1:COUNT_F], ALU.is_gt))
            link(nc.vector.tensor_reduce(falls[0:COUNT_P, 0:1], below[:, 0:COUNT_F - 1], AX.X, ALU.max))
            dve.wait_ge(next_in, 16)
            nc.vector.tensor_tensor(falls[0:COUNT_P - 1, 1:2], dst_f[0:COUNT_P - 1, COUNT_F - 1:COUNT_F],
                                    next_dst[0:COUNT_P - 1, :], ALU.is_gt).then_inc(falls_set, 1)
            dve.wait_ge(item_set, 1)
            link(nc.vector.tensor_scalar(starts[:, :], block_i[:, :], -0.5, None, ALU.add))
            dve.sem_inc(starts_set, 1)
            dve.wait_ge(falls_sum, 1)
            link(nc.vector.tensor_reduce(sum_f[:, 0:1], stage[2][:, 0:2], AX.X, ALU.add))
            nc.vector.tensor_copy(unsorted_i[:, :], sum_f[0:1, 0:1]).then_inc(order_known, 1)
            with if_unsorted(dve):
                sorted_ = [0]

                def step(ins, base=None):
                    sorted_[0] += 1
                    ins.then_inc(sort_chain, 1)
                    dve.wait_ge(sort_chain, sorted_[0] if base is None else base + sorted_[0])

                with dve.Fori(1, NB) as b:
                    nc.vector.tensor_scalar(below, dst_f, starts[0:COUNT_P, bass.ds(b, 1)], None, ALU.is_lt, ALU.add,
                                            accum_out=count[0:COUNT_P, bass.ds(b, 1)]).then_inc(sort_chain, 1)
                    dve.wait_ge(sort_chain, b)
                sorted_[0] = NB - 1
                dve.sem_inc(sort_count, 1)
                dve.wait_ge(ranked, 1)
                step(nc.vector.tensor_copy(filled_to, stage[0][:, 0:NB]))
                for a in range(3):
                    step(nc.vector.memset(lists_at[:, a:a + 1], float(a * E)))
                step(nc.vector.memset(reached, 0.0))
                lead, per_row = sorted_[0], 8

                def place_edges(r, n):
                    base = r * per_row + lead
                    sorted_[0] = 0
                    dve.wait_ge(edge_in, r * 48 + 48)
                    step(nc.vector.tensor_copy(dst_e[0:n, :], edge_e[0:n, 1:2]), base)
                    step(nc.vector.tensor_scalar(reached[0:n, 0:NB], starts[0:n, :], dst_e[0:n, :], None, ALU.is_lt), base)
                    nc.vector.tensor_tensor(inside[0:n, :], reached[0:n, 0:NB], reached[0:n, 1:NB + 1], ALU.subtract).then_inc(inside_set, 1)
                    dve.wait_ge(inside_set, r + 1)
                    dve.wait_ge(ranked, r + 2)
                    step(nc.vector.tensor_tensor(rank[0:n, :], filled_to[0:n, :], stage[0][0:n, 0:NB], ALU.add), base)
                    step(nc.vector.tensor_tensor(rank[0:n, :], rank[0:n, :], inside[0:n, :], ALU.mult), base)
                    step(nc.vector.tensor_reduce(place[0:n, :], rank[0:n, :], AX.X, ALU.add), base)
                    step(nc.vector.tensor_tensor(filled_to, filled_to, stage[1][:, 0:NB], ALU.add), base)
                    step(nc.vector.tensor_scalar(rank[0:n, 0:3], lists_at[0:n, :], place[0:n, :], None, ALU.add), base)
                    dve.wait_ge(row_sorted, r + 1)
                    step(nc.vector.tensor_copy(place_i[0:n, :], rank[0:n, 0:3]), base)
                    dve.sem_inc(placed, 1)
                    assert sorted_[0] == per_row
                each_row(dve, place_edges)
                dve.wait_ge(resorted, 16 * 7)
            dve.wait_ge(src_in, 48)
            nc.vector.tensor_copy(src_f, src_rows).then_inc(src_done, 1)
            nc.vector.tensor_scalar(low, src_rows, P - 1, None, ALU.bitwise_and).then_inc(src_split, 1)
            nc.vector.tensor_scalar(high, src_rows, 7, None, ALU.arith_shift_right).then_inc(src_split, 1)
            dve.wait_ge(src_split, 2)
            nc.vector.scalar_tensor_tensor(high.bitcast(F32), low, float(G), high, ALU.mult, ALU.add).then_inc(src_done, 1)
            for b in range(1, DVE_COUNTS):
                link(nc.vector.tensor_scalar(below, dst_f, float(BN * b), None, ALU.is_lt, ALU.add,
                                             accum_out=count[0:COUNT_P, b:b + 1]))
            dve.sem_inc(counted, 1)
            dve.wait_ge(iota_set, 1)
            nc.vector.tensor_copy(iota_p[:, :], iota_i)
            dve.wait_ge(signed, NB - DVE_COUNTS)
            nc.vector.tensor_scalar(count[0:COUNT_P, DVE_COUNTS:NB], below_act[0:COUNT_P, DVE_COUNTS:NB], 0.5, COUNT_F / 2,
                                    ALU.mult, ALU.add).then_inc(counted, 1)
            dve.wait_ge(edge_sum, 1)
            link(nc.vector.tensor_copy(edge_at[:, :], stage[2][:, 0:NB + 1]))
            link(nc.vector.tensor_copy(edge_i[:, :], edge_at[:, :]))
            link(nc.vector.tensor_scalar(row_i[:, :], edge_i[:, :], 7, None, ALU.arith_shift_right))
            link(nc.vector.tensor_copy(row_at[:, :], row_i[:, :]))
            link(nc.vector.tensor_scalar(last_f[:, :], edge_at[:, 1:NB + 1], -1.0, None, ALU.add))
            link(nc.vector.tensor_copy(last_i[:, :], last_f[:, :]))
            link(nc.vector.tensor_scalar(last_i[:, :], last_i[:, :], 7, None, ALU.arith_shift_right))
            link(nc.vector.tensor_copy(last_f[:, :], last_i[:, :]))
            link(nc.vector.tensor_tensor(filled[:, :], edge_at[:, 1:NB + 1], edge_at[:, 0:NB], ALU.is_gt))
            link(nc.vector.scalar_tensor_tensor(rows_of[:, :], last_f[:, :], 1.0, row_at[:, 0:NB], ALU.add, ALU.subtract))
            link(nc.vector.tensor_tensor(rows_of[:, :], rows_of[:, :], filled[:, :], ALU.mult))
            link(nc.vector.tensor_tensor_scan(item_at[:, 1:NB + 1], rows_of[:, :], zeros_b[:, :], 0.0, ALU.add, ALU.add))
            link(nc.vector.tensor_copy(item_at_i[:, :], item_at[0:1, :]))
            link(nc.vector.tensor_tensor(lag[:, :], row_at[:, 0:NB], item_at[:, 0:NB], ALU.subtract))
            link(nc.vector.tensor_tensor(slip[:, :], lag[:, 1:NB], lag[:, 0:NB - 1], ALU.subtract))
            dve.wait_ge(item_set, 2)
            link(nc.vector.tensor_copy(item_f[:, :], item_i[:, :]))
            wide = [P, SETS, NB - 1]
            link(nc.vector.tensor_tensor(begun, item_at[:, 1:NB].unsqueeze(1).to_broadcast(wide),
                                         item_f[:, :].unsqueeze(2).to_broadcast(wide), ALU.is_le))
            link(nc.vector.tensor_tensor(slips, begun, slip[:, :].unsqueeze(1).to_broadcast(wide), ALU.mult))
            link(nc.vector.tensor_reduce(block_f[:, :], begun, AX.X, ALU.add))
            link(nc.vector.tensor_reduce(shift[:, :], slips, AX.X, ALU.add))
            link(nc.vector.tensor_scalar(first_dst[:, :], block_f[:, :], float(BN), None, ALU.mult))
            link(nc.vector.tensor_tensor(row_f[:, :], item_f[:, :], shift[:, :], ALU.add))
            link(nc.vector.tensor_copy(row_of[:, :], row_f[:, :]))
            dve.sem_inc(rows_set, 1)
            link(nc.vector.tensor_scalar(regs_f[:, 0, :], block_f[:, :], float(SB), None, ALU.mult))
            link(nc.vector.tensor_scalar(row_f[:, :], row_f[:, :], float(ROWS - 1), None, ALU.min))
            link(nc.vector.tensor_scalar(regs_f[:, 2, :], row_f[:, :], 1.0, None, ALU.add))
            link(nc.vector.tensor_copy(held_i[:, :], row_f[:, :]))
            link(nc.vector.tensor_scalar(held_i[:, :], held_i[:, :], RING - 1, None, ALU.bitwise_and))
            nc.vector.tensor_scalar(regs_f[:, 1, :], held_i[:, :], float(D + 1), None, ALU.mult).then_inc(regs_ready, 1)
            for c in range(RING // CH):
                link(nc.vector.tensor_scalar(last_f[0:1, :], row_at[0:1, 0:NB], -1.0, float((c + 1) * CH), ALU.mult, ALU.add))
                link(nc.vector.tensor_tensor(last_f[0:1, :], last_f[0:1, :], rows_of[0:1, :], ALU.min))
                link(nc.vector.tensor_scalar(last_f[0:1, :], last_f[0:1, :], 0.0, None, ALU.max, ALU.add,
                                             accum_out=begun_by[:, c:c + 1]))
            nc.vector.tensor_copy(begun_by_i[:, :], begun_by[:, :]).then_inc(early_items, 1)
            with dve.Fori(0, SETS // BUFS) as some:
                for h in range(BUFS):
                    dve.wait_ge(rows_in[h], some * 16 + 16)
                    dve.wait_ge(tab_done, some * BUFS + (h + 1))
                    nc.vector.tensor_scalar(rowf[:, h, :], rows[:, h, 0, :], first_dst[:, bass.ds(some * BUFS + h, 1)], None,
                                            ALU.subtract).then_inc(row_done, 1)
            dve.wait_ge(tab_done, BUFS + SETS)
            dve.wait_ge(regs_in, 48)
            dve.wait_ge(total_set, 1)

            def columns(layer, at, chunk, h):
                nc.vector.tensor_copy(edge_c[:, h, :, :], edge_t[:, bass.ds(at, CH), :]).then_inc(cols_in, 1)
                dve.wait_ge(cols_in, chunk + (layer * (ITEMS // CH) + 1))

            def one_hot(j):
                c = edge_c[:, j // CH % 2, j % CH, :]
                nc.vector.tensor_scalar(hot[:, j % HOTS, :], iota_p[:, :], c[:, 0:1], c[:, 1:2],
                                        ALU.is_equal, ALU.mult).then_inc(hot_ready, 1)

            def add_layer(layer, to, degrees):
                width = D + 1 if degrees else D

                def body(turn, last):
                    i = turn * BODY + layer * ITEMS
                    for h in range(2):
                        groups = nc.values_load_multi_w_load_instructions(
                            item_regs[0:1, bass.ds(turn * BODY + h * CH, CH)], engines=[mybir.EngineType.DVE],
                            min_val=0, max_val=G - SB,
                            skip_runtime_bounds_check_because="a block's first group is below G by construction")[1]
                        for jj in range(CH):
                            j = h * CH + jj
                            ahead = j + LOOKAHEAD
                            if not (last and ahead >= BODY):
                                if ahead % CH == 0:
                                    columns(layer, turn * BODY + ahead, turn * 2 + ahead // CH, ahead // CH % 2)
                                if j % 2 == 0:
                                    dve.wait_ge(items_done, i + (ahead + 2))
                                one_hot(ahead)
                            if j % 2 == 0:
                                dve.wait_ge(items_done, i + (HOTS + j + 2))
                            dve.wait_ge(bank_free, i + (BANKS + j))
                            got = sums[j % BANKS][:, 0:SB * width].rearrange("p (g d) -> p g d", g=SB)
                            if degrees:
                                d = degree[:, bass.ds(groups[jj], SB)]
                                nc.vector.tensor_tensor(d, d, got[:, :, D], ALU.add).then_inc(deg_added, 1)
                            s = (nodes[:, to, bass.ds(groups[jj], SB), :] if isinstance(to, int) else
                                 nodes[:, bass.ds(to, 1), bass.ds(groups[jj], SB), :].rearrange("p l g d -> p (l g) d"))
                            nc.vector.tensor_tensor(s, s, got[:, :, 0:D], ALU.add).then_inc(bank_free, 1)

                columns(layer, 0, 0, 0)
                for k in range(LOOKAHEAD):
                    one_hot(k)
                with dve.Fori(0, ITEMS // BODY - 1) as turn:
                    body(turn, False)
                body(ITEMS // BODY - 1, True)
                dve.wait_ge(bank_free, (layer + 1) * ITEMS + BANKS)

            with dve.Fori(0, LIGHT - 1) as l:
                dve.wait_ge(cleared, l + 1)
                add_layer(l, l, False)
                nc.vector.tensor_tensor(nodes[:, TOTAL, :, :], nodes[:, TOTAL, :, :],
                                        nodes[:, bass.ds(l, 1), :, :].rearrange("p l g d -> p (l g) d"), ALU.add).then_inc(summed, 1)
                dve.wait_ge(summed, l + 1)
            add_layer(LIGHT - 1, TOTAL, False)

            def totals(l, first, last):
                def total(n, h):
                    dve.wait_ge(dense_done, n + (l * STEPS + 1))
                    gs = bass.ds(n * DB, DB)
                    nc.vector.tensor_tensor(nodes[:, TOTAL if l else XNODES, gs, :], nodes[:, XNODES, gs, :],
                                            sums[h][:, 0:DB * D].rearrange("p (g d) -> p g d", g=DB), ALU.add).then_inc(dense_out, 1)
                with dve.Fori(first // 2, last // 2) as two:
                    total(two * 2, 0)
                    total(two * 2 + 1, 1)
                if last % 2:
                    total(last - 1, 0)

            def norm(n):
                def wide(v, q):
                    return v.unsqueeze(2).to_broadcast([P, PART[q + 1] - PART[q], D])
                for q in range(Q):
                    gs = slice(PART[q], PART[q + 1])
                    if n == 1:
                        totals(1, PART[q] // DB, PART[q + 1] // DB)
                        dve.wait_ge(dense_out, 2 + STEPS + PART[q + 1] // DB)
                    link(nc.vector.tensor_reduce(sum_f[:, gs], nodes[:, TOTAL, gs, :], AX.X, ALU.add))
                    link(nc.vector.tensor_scalar(stage[2][:, gs], sum_f[:, gs], 1.0 / D, None, ALU.mult))
                    nc.vector.tensor_tensor(nodes[:, TOTAL, gs, :], nodes[:, TOTAL, gs, :], wide(stage[2][:, gs], q),
                                            ALU.subtract).then_inc(centred, 1)
                for q in range(Q):
                    gs = slice(PART[q], PART[q + 1])
                    dve.wait_ge(squared, n * Q + q + 1)
                    link(nc.vector.tensor_reduce(sum_f[:, gs], nodes[:, XNODES if n == 0 else 0, gs, :], AX.X, ALU.add))
                    nc.vector.tensor_scalar(rstd[:, gs], sum_f[:, gs], 1.0 / (D * (LIGHT + 1) ** 2) if n == 0 else 1.0 / D, EPS,
                                            ALU.mult, ALU.add).then_inc(var_set, 1)
                for q in range(Q):
                    gs = slice(PART[q], PART[q + 1])
                    dve.wait_ge(std_set, n * Q + q + 1)
                    link(nc.vector.reciprocal(stage[2][:, gs], rstd[:, gs]))
                    nc.vector.tensor_tensor(nodes[:, TOTAL, gs, :], nodes[:, TOTAL, gs, :], wide(stage[2][:, gs], q),
                                            ALU.mult).then_inc(normed, 1)

            norm(0)
            link(nc.vector.memset(edge_t[:, :, 1], 1.0))
            dve.wait_ge(cleared, 3)
            add_layer(LIGHT, 0, True)
            dve.wait_ge(deg_added, ITEMS)
            link(nc.vector.tensor_scalar(rdeg[:, :], degree[:, :], 1.0, None, ALU.max))
            nc.vector.reciprocal(rdeg[:, :], rdeg[:, :]).then_inc(degrees_known, 1)
            dve.wait_ge(self_out, 1 + STEPS)
            totals(0, 0, STEPS)
            dve.wait_ge(cleared, 4)
            add_layer(LIGHT + 1, 1, False)
            dve.wait_ge(self_out, 1 + 2 * STEPS)
            norm(1)


ARGS = ["x", "src", "dst", "edge_weight", "L1_gnn_W_self1", "L1_gnn_W_neigh1", "L1_gnn_b1",
        "L1_gnn_W_self2", "L1_gnn_W_neigh2", "L1_gnn_b2"]


def kernel(**inputs):
    import concourse.bacc as bacc
    from concourse.bass_utils import run_bass_kernel_spmd

    nc = bacc.Bacc("TRN2", target_bir_lowering=False, num_devices=1)
    arrays, args = {}, []
    for name in ARGS:
        a = np.ascontiguousarray(inputs[name])
        arrays[f"in_{name}"] = a
        args.append(nc.dram_tensor(f"in_{name}", a.shape, mybir.dt.from_np(a.dtype), kind="ExternalInput").ap())
    args.append(nc.dram_tensor("out", (N, D), F32, kind="ExternalOutput").ap())
    build_program(nc, *args)
    result = run_bass_kernel_spmd(nc, [arrays], core_ids=[0])
    return result.results[0]["out"]
```
